# Optimizing a Trainium2 kernel written in Bass

```python
import numpy as np
import jax
import jax.numpy as jnp

def _softmax(x, axis=-1):
    return jax.nn.softmax(x, axis=axis)

def _gelu(x):
    return jax.nn.gelu(x, approximate=True)

def _silu(x):
    return jax.nn.silu(x)

def _sigmoid(x):
    return jax.nn.sigmoid(x)

def _layernorm(x, axis=-1, eps=1e-05):
    m = jnp.mean(x, axis=axis, keepdims=True)
    v = jnp.var(x, axis=axis, keepdims=True)
    return (x - m) / jnp.sqrt(v + eps)

def _scatter_add(tgt, idx, src, axis=0):
    return tgt.at[idx].add(src)

def _segment_sum(src, seg, n):
    return jax.ops.segment_sum(src, seg, n)
kernel_name = 'mk_xattn_ffn_d1_seqx_r8_11ee33'

def setup_inputs(seed: int=0):
    np.random.seed(seed)
    _w = jnp.asarray

    def _rec_inputs():
        import jax
        import jax.numpy as jnp
        _rk = jax.random.key(seed)
        x = -0.0003929 + 0.9999 * jax.random.normal(jax.random.fold_in(_rk, 1), (16, 64, 128), jnp.float32)
        _lenS = 64 - jax.random.randint(jax.random.fold_in(_rk, 7), (16,), 0, max(1, 64 // 4) + 1, jnp.int32)
        _lenS2 = 64 - jax.random.randint(jax.random.fold_in(_rk, 8), (16,), 0, max(1, 64 // 4) + 1, jnp.int32)
        _ctx_1024P = jax.random.normal(jax.random.fold_in(_rk, 11), (16, 16, 128), jnp.float32)
        _ctx_1024c = jax.random.dirichlet(jax.random.fold_in(_rk, 511), 0.3 * jnp.ones((16,), jnp.float32), (16, 64))
        _ctx_1024t = jnp.einsum('bsk,bkd->bsd', _ctx_1024c, _ctx_1024P)
        _ctx_1024t = _ctx_1024t * jax.lax.rsqrt(jnp.mean(jnp.square(_ctx_1024t)) + 1e-12) * 0.953939
        ctx_1024 = 2.81802e-05 + 1.00001 * (_ctx_1024t + 0.3 * jax.random.normal(jax.random.fold_in(_rk, 611), (16, 64, 128), jnp.float32))
        return (x, ctx_1024)
    x, ctx_1024 = _rec_inputs()

    def _L0_xattn_setup():
        import jax, jax.numpy as jnp
        import numpy as np
        key = jax.random.key(seed)
        ks = jax.random.split(key, 9)
        B, S, D = (8, 256, 128)
        Qd = Kd = Vd = 128
        s = 1.0 / np.sqrt(D)
        return {'query': jax.random.normal(ks[0], (B, S, D), jnp.float32), 'key': jax.random.normal(ks[1], (B, S, D), jnp.float32), 'value': jax.random.normal(ks[2], (B, S, D), jnp.float32), 'Wq': jax.random.normal(ks[3], (D, Qd), jnp.float32) * s, 'bq': jnp.zeros((Qd,), jnp.float32), 'Wk': jax.random.normal(ks[4], (D, Kd), jnp.float32) * s, 'bk': jnp.zeros((Kd,), jnp.float32), 'Wv': jax.random.normal(ks[5], (D, Vd), jnp.float32) * s, 'bv': jnp.zeros((Vd,), jnp.float32)}
    _L0_xattn_all = _L0_xattn_setup()
    _L0_xattn_in = {k: v for k, v in _L0_xattn_all.items() if k in ('Wq', 'bq', 'Wk', 'bk', 'Wv', 'bv')}
    del _L0_xattn_all

    def _L0_ffn_setup():
        import jax, jax.numpy as jnp
        import numpy as np
        D = 128
        H = 128
        E = 8
        K = 2
        I = 2 * 128
        ROUTE_SCALE = 1.0
        key = jax.random.key(seed)
        ks = jax.random.split(key, 12)
        s = lambda *sh: 1.0 / np.sqrt(sh[-1])
        return {'x': jax.random.normal(ks[0], (1, 256, D), jnp.float32), 'gate_w': jax.random.normal(ks[1], (E, D), jnp.float32) * s(E, D), 'w1': jax.random.normal(ks[2], (E, H, D), jnp.float32) * s(H, D), 'b1': jax.random.normal(ks[3], (E, H), jnp.float32) * 0.01, 'w2': jax.random.normal(ks[4], (E, D, H), jnp.float32) * s(D, H), 'b2': jax.random.normal(ks[5], (E, D), jnp.float32) * 0.01, 'w3': jax.random.normal(ks[6], (E, H, D), jnp.float32) * s(H, D), 'b3': jax.random.normal(ks[7], (E, H), jnp.float32) * 0.01, 'sw1': jax.random.normal(ks[8], (I, D), jnp.float32) * s(I, D), 'sw2': jax.random.normal(ks[9], (I, D), jnp.float32) * s(I, D), 'sw3': jax.random.normal(ks[10], (D, I), jnp.float32) * s(D, I)}
    _L0_ffn_all = _L0_ffn_setup()
    _L0_ffn_in = {k: v for k, v in _L0_ffn_all.items() if k in ('gate_w', 'w1', 'b1', 'w2', 'b2', 'w3', 'b3', 'sw1', 'sw2', 'sw3')}
    del _L0_ffn_all
    return {'x': x, 'ctx_1024': ctx_1024, 'L0_xattn_Wq': _L0_xattn_in['Wq'], 'L0_xattn_bq': _L0_xattn_in['bq'], 'L0_xattn_Wk': _L0_xattn_in['Wk'], 'L0_xattn_bk': _L0_xattn_in['bk'], 'L0_xattn_Wv': _L0_xattn_in['Wv'], 'L0_xattn_bv': _L0_xattn_in['bv'], 'L0_ffn_gate_w': _L0_ffn_in['gate_w'], 'L0_ffn_w1': _L0_ffn_in['w1'], 'L0_ffn_b1': _L0_ffn_in['b1'], 'L0_ffn_w2': _L0_ffn_in['w2'], 'L0_ffn_b2': _L0_ffn_in['b2'], 'L0_ffn_w3': _L0_ffn_in['w3'], 'L0_ffn_b3': _L0_ffn_in['b3'], 'L0_ffn_sw1': _L0_ffn_in['sw1'], 'L0_ffn_sw2': _L0_ffn_in['sw2'], 'L0_ffn_sw3': _L0_ffn_in['sw3']}

def reference(x, ctx_1024, L0_xattn_Wq, L0_xattn_bq, L0_xattn_Wk, L0_xattn_bk, L0_xattn_Wv, L0_xattn_bv, L0_ffn_gate_w, L0_ffn_w1, L0_ffn_b1, L0_ffn_w2, L0_ffn_b2, L0_ffn_w3, L0_ffn_b3, L0_ffn_sw1, L0_ffn_sw2, L0_ffn_sw3):
    import jax
    import jax.numpy as jnp

    def _L0_xattn_ref(query, key, value, Wq, bq, Wk, bk, Wv, bv):
        import jax, jax.numpy as jnp
        import numpy as np
        Q = jnp.einsum('bsd,de->bse', query, Wq) + bq
        K = jnp.einsum('bsd,de->bse', key, Wk) + bk
        V = jnp.einsum('bsd,de->bse', value, Wv) + bv
        scale = 1.0 / jnp.sqrt(jnp.asarray(K.shape[-1], Q.dtype))
        scores = jnp.einsum('bqe,bke->bqk', Q, K) * scale
        attn = jax.nn.softmax(scores, axis=-1)
        return jnp.einsum('bqk,bkv->bqv', attn, V)

    def _L0_ffn_ref(x, gate_w, w1, b1, w2, b2, w3, b3, sw1, sw2, sw3):
        import jax, jax.numpy as jnp
        import numpy as np
        D = 128
        H = 128
        E = 8
        K = 2
        I = 2 * 128
        ROUTE_SCALE = 1.0
        B, S, _ = x.shape
        xt = x.reshape(-1, D)
        logits = xt @ gate_w.T
        scores = jax.nn.softmax(logits.astype(jnp.float32), axis=-1)
        top_vals, idx = jax.lax.top_k(scores, K)
        weights = jnp.take_along_axis(scores, idx, axis=1).astype(x.dtype) * ROUTE_SCALE
        xs = xt[:, None, :] * weights[:, :, None]
        y = jnp.zeros_like(xt)
        for e in range(E):
            mask = (idx == e).astype(x.dtype)
            h = jax.nn.silu(jnp.einsum('tkd,hd->tkh', xs, w1[e]) + b1[e])
            x2 = jnp.einsum('tkh,dh->tkd', h, w2[e]) + b2[e]
            x3 = jnp.einsum('tkd,hd->tkh', xs, w3[e]) + b3[e]
            y = y + jnp.sum(x2 * x3 * mask[:, :, None], axis=1)
        z = jax.nn.silu(xt @ sw1.T) * (xt @ sw2.T) @ sw3.T
        return (y + z).reshape(B, S, D)
    x = x + _L0_xattn_ref(_layernorm(x, axis=-1), ctx_1024, ctx_1024, L0_xattn_Wq, L0_xattn_bq, L0_xattn_Wk, L0_xattn_bk, L0_xattn_Wv, L0_xattn_bv)
    x = x + _L0_ffn_ref(_layernorm(x, axis=-1), L0_ffn_gate_w, L0_ffn_w1, L0_ffn_b1, L0_ffn_w2, L0_ffn_b2, L0_ffn_w3, L0_ffn_b3, L0_ffn_sw1, L0_ffn_sw2, L0_ffn_sw3)
    return x

_drawn_inputs = setup_inputs


def setup_inputs(seed=0):
    import zlib

    import numpy as np

    out = dict(_drawn_inputs(seed))
    spreads = {'L0_xattn_bq': (0.0, 0.371), 'L0_xattn_bk': (0.0, 2.0), 'L0_xattn_bv': (0.0, 0.1)}
    factors = {'L0_ffn_b1': 31.542, 'L0_ffn_b2': 8.0, 'L0_ffn_b3': 27.345}
    for name, (base, spread) in spreads.items():
        noise = np.random.default_rng([zlib.crc32(name.encode()), seed]).standard_normal(out[name].shape)
        drawn = base * np.exp(spread * noise) if base else spread * noise
        out[name] = jnp.asarray(drawn.astype(out[name].dtype))
    for name, factor in factors.items():
        out[name] = (out[name] * factor).astype(out[name].dtype)
    return out
```

```python
from contextlib import ExitStack

import concourse.bass as bass
from concourse import mybir

F32 = mybir.dt.float32
F32R = mybir.dt.float32r
BF16 = mybir.dt.bfloat16
ALU = mybir.AluOpType
ACT = mybir.ActivationFunctionType
AX_X = mybir.AxisListType.X

P = 128
EPS = 1e-5
DMA = 16
COL_BQ, COL_BK = 0, 1
PARTS, PART_ROWS = 3, 32


def xattn_moe_ffn_kernel(nc, x, ctx_t, wq, wk, wv, cols, bv, gate_t, sw12_t, sw3_t,
                         w13_t, w2_t, b3_rows, ident, onehots, rank_weight, out_t):
    T = ctx_t.shape[1]
    NT = T // P
    G = 2
    HALF = T // G
    TH = NT // G
    S = 64
    E = w2_t.shape[0]
    C = sw3_t.shape[0]
    PAIRS = E // 2
    SCALE = 1.0 / float(P) ** 0.5
    assert P == 128 and HALF == 512 and C == 2 and E == 8

    with ExitStack() as ctx:
        def sb(name, shape, dt=F32):
            return ctx.enter_context(nc.sbuf_tensor(name, shape, dt))

        def sem(name):
            return ctx.enter_context(nc.semaphore(name))

        x_sb = sb("x_sb", [P, NT, P])
        ctx_sb = sb("ctx_sb", [P, T])
        wq_sb, wk_sb, wv_sb = sb("wq_sb", [P, P]), sb("wk_sb", [P, P]), sb("wv_sb", [P, P])
        cols_sb = sb("cols_sb", [P, 2])
        bv_sb = sb("bv_sb", [P, P])
        gate_sb = sb("gate_sb", [P, E])
        sw12_sb = sb("sw12_sb", [P, 2 * C, P])
        sw3_sb = sb("sw3_sb", [P, C, P])
        b3_sb = sb("b3_sb", [P, P])
        ident_sb = sb("ident_sb", [P, P])
        onehots_sb = sb("onehots_sb", [P, 2 * E])
        rank_sb = sb("rank_sb", [P, E])
        ident_bf = sb("ident_bf", [P, P], BF16)

        stats = sb("stats", [P, 2, NT, 6])
        mean_var = sb("mean_var", [P, 2, NT, 2])
        var_eps = sb("var_eps", [P, 2, NT])
        rstd = sb("rstd", [P, 2, NT])
        minus_half = sb("minus_half", [P, NT])
        xn1 = sb("xn1", [P, NT, P])
        xn1_t = sb("xn1_t", [P, T])
        q_t, k_t = sb("q_t", [P, T]), sb("k_t", [P, T])
        v_sb = sb("v_sb", [P, NT, P])
        x_bv = sb("x_bv", [P, NT, P])
        score_max = sb("score_max", [P, NT])
        shifted = sb("shifted", [P, NT, S])
        probs = sb("probs", [P, NT, P])
        probs_t = sb("probs_t", [P, NT, P])
        prob_sum = sb("prob_sum", [P, NT])
        prob_rsum = sb("prob_rsum", [P, NT])
        x2 = sb("x2", [P, NT, P])
        xn2 = sb("xn2", [P, NT, P])
        x2_t = sb("x2_t", [P, T])
        xn2_t = sb("xn2_t", [P, T])

        small = {n: sb("route_" + n, [P, NT, E]) for n in (
            "shifted", "exp", "score", "eq", "key", "first", "rest", "second", "mask", "masked", "r1", "r2")}
        per_tile = {n: sb("route_" + n, [P, NT]) for n in (
            "lmax", "sum", "rsum", "max1", "key1", "max2", "key2")}
        route = sb("route", [P, NT, P], BF16)
        route_t = sb("route_t", [P, T], BF16)
        pick_score = sb("pick_score", [P, E, P], BF16)
        pick_b3 = sb("pick_b3", [P, E, P], BF16)
        b3_part = sb("b3_part", [P, P], BF16)
        b3_q1 = sb("b3_q1", [P, P], BF16)
        b3_r1 = sb("b3_r1", [P, P])
        b3_q2 = sb("b3_q2", [P, P], BF16)
        b3_r2 = sb("b3_r2", [P, P])

        gate_act = sb("gate_act", [P, C, HALF])
        gated = sb("gated", [P, C, HALF])
        z_t = sb("z_t", [P, T])
        y_t = sb("y_t", [P, T])

        w13_raw = [sb(f"w13_raw{p}", [P, 2, P]) for p in range(2)]
        w13_hi = [sb(f"w13_hi{p}", [P, 2, P], F32R) for p in range(2)]
        w13_lo = [sb(f"w13_lo{p}", [P, 2, P], F32R) for p in range(2)]
        w2_sb = [sb(f"w2_sb{p}", [P, P + 2]) for p in range(2)]
        xs = [sb(f"xs{h}", [P, HALF]) for h in range(G)]
        xs_hi = [sb(f"xs_hi{h}", [P, HALF], F32R) for h in range(G)]
        xs_lo = [sb(f"xs_lo{h}", [P, HALF], F32R) for h in range(G)]
        hidden = [sb(f"hidden{h}", [P, HALF]) for h in range(G)]
        x3 = [sb(f"x3{h}", [P, HALF]) for h in range(G)]
        prod = [sb(f"prod{h}", [P, HALF]) for h in range(G)]

        bank = [ctx.enter_context(nc.psum_tensor(f"bank{i}", [P, 512], F32)) for i in range(8)]
        ps_k = ps_q = ps_x2t = ps_z = ps_a1 = [bank[0], bank[1]]
        ps_v = ps_av = ps_a3 = [bank[2], bank[3]]
        ps_xn1t = ps_pt = ps_xn2t = ps_a2 = [bank[4], bank[5]]
        ps_scores = ps_bcast = [bank[6], bank[7]]
        ps_logits = bank[7][:, 0:NT * E].rearrange("p (t e) -> p t e", e=E)
        ps_route_t = bank[7][:, :].bitcast(BF16)
        ps_gate = lambda g, c: bank[g] if c == 0 else bank[6]
        ps_up = lambda g, c: bank[2 + g] if c == 0 else bank[4 + g]

        ld = {n: sem("ld_" + n) for n in (
            "x0", "x1", "ctx0", "ctx1", "wq", "wk", "wv", "cols", "bv", "gate", "sw12", "sw3",
            "b3", "ident", "onehots", "rank")}
        ld_w13 = [sem(f"ld_w13_{p}") for p in range(2)]
        ld_w2 = [sem(f"ld_w2_{p}") for p in range(2)]
        stored = sem("stored")
        (kt_mm, v_mm, xn1t_mm, q_mm, scores_mm, pt_mm, av_mm, x2t_mm, xn2t_mm, logits_mm,
         gate_mm, up_mm, route_mm, bcast_mm, a1_mm, a3_mm, a2_mm) = (sem(n) for n in (
            "kt_mm", "v_mm", "xn1t_mm", "q_mm", "scores_mm", "pt_mm", "av_mm", "x2t_mm", "xn2t_mm", "logits_mm",
            "gate_mm", "up_mm", "route_mm", "bcast_mm", "a1_mm", "a3_mm", "a2_mm"))
        (kt_out, v_out, xn1t_out, q_out, exps, pt_out, x2t_out, xn2t_out, route_exp, silus,
         route_out, x3_out, xs_hi_out, w_hi_out, picks_score, ident_cast) = (sem(n) for n in (
            "kt_out", "v_out", "xn1t_out", "q_out", "exps", "pt_out", "x2t_out", "xn2t_out", "route_exp", "silus",
            "route_out", "x3_out", "xs_hi_out", "w_hi_out", "picks_score", "ident_cast"))
        (stat_dve, var_ready, xn1_ready, smax_ready, shift_ready, psum_ready, rsum_ready, x2_ready, xn2_ready,
         route_step, route_shift, route_rows, gated_ready, xs_out, xs_lo_out, prod_out) = (sem(n) for n in (
            "stat_dve", "var_ready", "xn1_ready", "smax_ready", "shift_ready", "psum_ready", "rsum_ready", "x2_ready",
            "xn2_ready", "route_step", "route_shift", "route_rows", "gated_ready", "xs_out", "xs_lo_out", "prod_out"))
        (consts_ready, zeros_ready, var_eps_out, rstd_out, xbv_out, b3_step, pick_b3_ready, w_lo_out, y_out) = (
            sem(n) for n in (
                "consts_ready", "zeros_ready", "var_eps_out", "rstd_out", "xbv_out", "b3_step", "pick_b3_ready",
                "w_lo_out", "y_out"))

        tok = lambda g: slice(g * HALF, (g + 1) * HALF)
        tile = lambda t: slice(t * P, (t + 1) * P)
        tiles = lambda g: slice(g * TH, (g + 1) * TH)
        in_half = lambda t: slice((t % TH) * P, (t % TH + 1) * P)

        x_rows = x.rearrange("(t p) d -> p t d", p=P)

        block = ctx.enter_context(nc.Block())

        @block.sync
        def _(sp):
            sp.dma_start(x_sb[:, tiles(0), :], x_rows[:, tiles(0), :]).then_inc(ld["x0"], DMA)
            sp.dma_start(wk_sb[:], wk).then_inc(ld["wk"], DMA)
            sp.dma_start(ctx_sb[:, tok(0)], ctx_t[:, tok(0)]).then_inc(ld["ctx0"], DMA)
            sp.dma_start(x_sb[:, tiles(1), :], x_rows[:, tiles(1), :]).then_inc(ld["x1"], DMA)
            sp.dma_start(ctx_sb[:, tok(1)], ctx_t[:, tok(1)]).then_inc(ld["ctx1"], DMA)
            sp.dma_start(b3_sb[:], b3_rows).then_inc(ld["b3"], DMA)
            sp.dma_start(gate_sb[:], gate_t).then_inc(ld["gate"], DMA)
            sp.dma_start(rank_sb[:], rank_weight.partition_broadcast(P)).then_inc(ld["rank"], DMA)
            sp.dma_start(sw12_sb[:], sw12_t).then_inc(ld["sw12"], DMA)
            sp.dma_start(sw3_sb[:], sw3_t.rearrange("c h d -> h c d")).then_inc(ld["sw3"], DMA)
            for p in range(2):
                sp.dma_start(w13_raw[p][:], w13_t[p]).then_inc(ld_w13[p], DMA)
                sp.dma_start(w2_sb[p][:], w2_t[p]).then_inc(ld_w2[p], DMA)
            with sp.Fori(0, PAIRS - 1) as i:
                for p in range(2):
                    sp.wait_ge(w_lo_out, 2 * i + p + 1)
                    sp.dma_start(w13_raw[p][:], w13_t[bass.ds(2 * i + p + 2, 1)].rearrange("o d c h -> (o d) c h")
                                 ).then_inc(ld_w13[p], DMA)
                    sp.wait_ge(prod_out, G + 4 * i + 2 * p + 2)
                    sp.dma_start(w2_sb[p][:], w2_t[bass.ds(2 * i + p + 2, 1)].rearrange("o h d -> (o h) d")
                                 ).then_inc(ld_w2[p], DMA)
            for h in range(G):
                sp.wait_ge(y_out, G + 2 * (E - 1) + h + 1)
                sp.dma_start(out_t[:, tok(h)], y_t[:, tok(h)]).then_inc(stored, DMA)
            sp.wait_ge(stored, DMA * G)

        @block.gpsimd
        def _(pool):
            nc.gpsimd.memset(minus_half[:], -0.5).then_inc(consts_ready, 1)
            nc.gpsimd.memset(probs[:], 0.0).then_inc(zeros_ready, 1)
            nc.gpsimd.memset(route[:], 0.0).then_inc(zeros_ready, 1)

            def rsqrt_var(norm, g):
                pool.wait_ge(var_ready, G * norm + g + 1)
                nc.gpsimd.tensor_scalar(var_eps[:, norm, tiles(g)], mean_var[:, norm, tiles(g), 1], EPS, None,
                                        ALU.add).then_inc(var_eps_out, 1)
                pool.wait_ge(var_eps_out, G * norm + g + 1)
                pool.wait_ge(consts_ready, 1)
                nc.gpsimd.tensor_tensor(rstd[:, norm, tiles(g)], var_eps[:, norm, tiles(g)], minus_half[:, tiles(g)],
                                        ALU.pow).then_inc(rstd_out, 1)

            rsqrt_var(0, 0)
            rsqrt_var(0, 1)
            pool.wait_ge(ld["bv"], DMA)
            for g in range(G):
                pool.wait_ge(ld[f"x{g}"], DMA)
                nc.gpsimd.tensor_tensor(x_bv[:, tiles(g), :], x_sb[:, tiles(g), :],
                                        bv_sb[:, :].unsqueeze(1).to_broadcast([P, TH, P]), ALU.add
                                        ).then_inc(xbv_out, 1)
            pool.wait_ge(ld["b3"], DMA)
            nc.gpsimd.tensor_copy(b3_q1[:], b3_sb[:]).then_inc(b3_step, 1)
            pool.wait_ge(b3_step, 1)
            nc.gpsimd.tensor_tensor(b3_r1[:], b3_sb[:], b3_q1[:], ALU.subtract).then_inc(b3_step, 1)
            pool.wait_ge(b3_step, 2)
            nc.gpsimd.tensor_copy(b3_q2[:], b3_r1[:]).then_inc(b3_step, 1)
            pool.wait_ge(b3_step, 3)
            nc.gpsimd.tensor_tensor(b3_r2[:], b3_r1[:], b3_q2[:], ALU.subtract).then_inc(b3_step, 1)
            pool.wait_ge(b3_step, 4)
            nc.gpsimd.tensor_copy(b3_part[:], b3_r2[:]).then_inc(b3_step, 1)
            pool.wait_ge(b3_step, 5)
            nc.gpsimd.tensor_copy(b3_part[0:PART_ROWS, :], b3_q1[0:PART_ROWS, :]).then_inc(b3_step, 1)
            nc.gpsimd.tensor_copy(b3_part[PART_ROWS:2 * PART_ROWS, :], b3_q2[PART_ROWS:2 * PART_ROWS, :]
                                  ).then_inc(b3_step, 1)
            pool.wait_ge(b3_step, 7)
            pool.wait_ge(ld["onehots"], DMA)
            nc.gpsimd.tensor_tensor(pick_b3[:], b3_part[:, :].unsqueeze(1).to_broadcast([P, E, P]),
                                    onehots_sb[:, E:2 * E].unsqueeze(2).to_broadcast([P, E, P]), ALU.mult
                                    ).then_inc(pick_b3_ready, 1)
            rsqrt_var(1, 0)
            rsqrt_var(1, 1)

            def split_low(e, p, i):
                pool.wait_ge(w_hi_out, e + 1)
                nc.gpsimd.tensor_tensor(w13_lo[p][:], w13_raw[p][:], w13_hi[p][:].bitcast(F32), ALU.subtract
                                        ).then_inc(w_lo_out, 1)

            split_low(0, 0, 0)
            for g in range(G):
                pool.wait_ge(prod_out, g + 1)
                pool.wait_ge(x2t_out, g + 1)
                nc.gpsimd.tensor_tensor(y_t[:, tok(g)], x2_t[:, tok(g)], z_t[:, tok(g)], ALU.add).then_inc(y_out, 1)

            def add_pair(i, last):
                for p in range(2):
                    for h in range(G):
                        s = 4 * i + 2 * p + h
                        if h == 1 and not (last and p == 1):
                            split_low(2 * i + p + 1, 1 - p, i)
                        pool.wait_ge(prod_out, G + s + 1)
                        pool.wait_ge(y_out, s + 1)
                        nc.gpsimd.tensor_tensor(y_t[:, tok(h)], y_t[:, tok(h)], prod[h][:], ALU.add
                                                ).then_inc(y_out, 1)

            with pool.Fori(0, PAIRS - 1) as i:
                add_pair(i, False)
            add_pair(PAIRS - 1, True)

        @block.scalar
        def _(act):
            act.dma_start(ident_sb[:], ident).then_inc(ld["ident"], DMA)
            act.dma_start(cols_sb[:], cols).then_inc(ld["cols"], DMA)
            act.dma_start(wv_sb[:], wv).then_inc(ld["wv"], DMA)
            act.dma_start(wq_sb[:], wq).then_inc(ld["wq"], DMA)
            act.dma_start(bv_sb[:], bv.partition_broadcast(P)).then_inc(ld["bv"], DMA)
            act.dma_start(onehots_sb[:], onehots).then_inc(ld["onehots"], DMA)
            act.wait_ge(ld["ident"], DMA)
            nc.scalar.activation(ident_bf[:], ident_sb[:], ACT.Copy).then_inc(ident_cast, 1)
            act.wait_ge(ld["cols"], DMA)

            def evac_k(g):
                act.wait_ge(kt_mm, g + 1)
                nc.scalar.activation(k_t[:, tok(g)], ps_k[g][:], ACT.Identity, bias=cols_sb[:, COL_BK:COL_BK + 1]
                                     ).then_inc(kt_out, 1)

            def evac_v(g):
                act.wait_ge(v_mm, g + 1)
                nc.scalar.activation(v_sb[:, tiles(g), :], ps_v[g][:].rearrange("p (t d) -> p t d", d=P), ACT.Copy
                                     ).then_inc(v_out, 1)

            def evac_xn1t(g):
                act.wait_ge(xn1t_mm, g + 1)
                nc.scalar.activation(xn1_t[:, tok(g)], ps_xn1t[g][:], ACT.Copy).then_inc(xn1t_out, 1)

            def evac_q(g):
                act.wait_ge(q_mm, g + 1)
                nc.scalar.activation(q_t[:, tok(g)], ps_q[g][:], ACT.Identity, bias=cols_sb[:, COL_BQ:COL_BQ + 1]
                                     ).then_inc(q_out, 1)

            evac_k(0)
            evac_v(0)
            evac_k(1)
            evac_xn1t(0)
            evac_v(1)
            evac_q(0)
            evac_xn1t(1)
            evac_q(1)
            act.wait_ge(ld["onehots"], DMA)
            nc.scalar.activation(pick_score[:], onehots_sb[:, 0:E].unsqueeze(2).to_broadcast([P, E, P]), ACT.Copy
                                 ).then_inc(picks_score, 1)

            act.wait_ge(zeros_ready, 1)
            for g in range(G):
                act.wait_ge(shift_ready, g + 1)
                for b in range(2):
                    rows = slice(b * S, (b + 1) * S)
                    nc.scalar.activation(probs[rows, tiles(g), rows], shifted[rows, tiles(g), :], ACT.Exp,
                                         scale=SCALE).then_inc(exps, 1)
            for g in range(G):
                act.wait_ge(pt_mm, g + 1)
                nc.scalar.activation(probs_t[:, tiles(g), :], ps_pt[g][:].rearrange("p (t d) -> p t d", d=P), ACT.Copy
                                     ).then_inc(pt_out, 1)
            for g in range(G):
                act.wait_ge(xn2t_mm, g + 1)
                nc.scalar.activation(xn2_t[:, tok(g)], ps_xn2t[g][:], ACT.Copy).then_inc(xn2t_out, 1)
                act.wait_ge(x2t_mm, g + 1)
                nc.scalar.activation(x2_t[:, tok(g)], ps_x2t[g][:], ACT.Copy).then_inc(x2t_out, 1)
            act.wait_ge(route_shift, 1)
            nc.scalar.activation(small["exp"][:], small["shifted"][:], ACT.Exp).then_inc(route_exp, 1)

            def split_high(e, p, loads):
                act.wait_ge(ld_w13[p], loads)
                nc.scalar.activation(w13_hi[p][:], w13_raw[p][:], ACT.Copy).then_inc(w_hi_out, 1)

            def shared_silu(g, c):
                act.wait_ge(gate_mm, C * g + c + 1)
                if g >= 1:
                    act.wait_ge(gated_ready, C * (g - 1) + c + 1)
                nc.scalar.activation(gate_act[:, c, :], ps_gate(g, c)[:], ACT.Silu).then_inc(silus, 1)

            shared_silu(0, 0)
            shared_silu(0, 1)
            split_high(0, 0, DMA)
            shared_silu(1, 0)
            act.wait_ge(route_mm, 1)
            nc.scalar.activation(route_t[:], ps_route_t, ACT.Copy).then_inc(route_out, 1)
            shared_silu(1, 1)

            def round_xs(s, h):
                act.wait_ge(xs_out, s + 1)
                nc.scalar.activation(xs_hi[h][:], xs[h][:], ACT.Copy).then_inc(xs_hi_out, 1)

            round_xs(0, 0)
            round_xs(1, 1)

            def expert_pair(i, last):
                for p in range(2):
                    e = 2 * i + p
                    for h in range(G):
                        s = 4 * i + 2 * p + h
                        if h == 0:
                            act.wait_ge(ld_w2[p], DMA * (i + 1))
                        act.wait_ge(a1_mm, s + 1)
                        act.wait_ge(a2_mm, s + 1)
                        nc.scalar.activation(hidden[h][:], ps_a1[h][:], ACT.Silu,
                                             bias=w2_sb[p][:, P:P + 1]).then_inc(silus, 1)
                        act.wait_ge(a3_mm, s + 1)
                        act.wait_ge(prod_out, s + 1)
                        nc.scalar.activation(x3[h][:], ps_a3[h][:], ACT.Copy).then_inc(x3_out, 1)
                        if h == 0 and not (last and p == 1):
                            act.wait_ge(a2_mm, G + 2 * e)
                            split_high(e + 1, 1 - p, DMA * (i + 1 + p))
                        if not (last and p == 1):
                            round_xs(s + 2, h)

            with act.Fori(0, PAIRS - 1) as i:
                expert_pair(i, False)
            expert_pair(PAIRS - 1, True)

        @block.vector
        def _(dve):
            def stats_of(norm, t, src):
                nc.vector.bn_stats(stats[:, norm, t, :], src[:, t, :]).then_inc(stat_dve, 1)

            def aggregate(norm, t):
                dve.wait_ge(stat_dve, norm * NT + t + 1)
                ins = nc.vector.bn_aggr(mean_var[:, norm, t, :], stats[:, norm, t, :])
                if t % TH == TH - 1:
                    ins.then_inc(var_ready, 1)

            def normalise(norm, t, src, dst, ready):
                nc.vector.tensor_scalar(dst[:, t, :], src[:, t, :], mean_var[:, norm, t, 0:1],
                                        rstd[:, norm, t:t + 1], ALU.subtract, ALU.mult).then_inc(ready, 1)

            for g in range(G):
                dve.wait_ge(ld[f"x{g}"], DMA)
                for t in range(g * TH, (g + 1) * TH):
                    stats_of(0, t, x_sb)
                for t in range(g * TH, (g + 1) * TH):
                    aggregate(0, t)
            for g in range(G):
                dve.wait_ge(rstd_out, g + 1)
                for t in range(g * TH, (g + 1) * TH):
                    normalise(0, t, x_sb, xn1, xn1_ready)

            for g in range(G):
                scores = ps_scores[g][:, 0:TH * S].rearrange("p (t k) -> p t k", k=S)
                dve.wait_ge(scores_mm, g + 1)
                nc.vector.reduce_max(score_max[:, tiles(g)], scores, AX_X).then_inc(smax_ready, 1)
                dve.wait_ge(smax_ready, g + 1)
                nc.vector.tensor_tensor(shifted[:, tiles(g), :], scores,
                                        score_max[:, tiles(g)].unsqueeze(2).to_broadcast([P, TH, S]),
                                        ALU.subtract).then_inc(shift_ready, 1)
            for g in range(G):
                for b in range(2):
                    rows = slice(b * S, (b + 1) * S)
                    dve.wait_ge(exps, 2 * g + b + 1)
                    nc.vector.reduce_sum(prob_sum[rows, tiles(g)], probs[rows, tiles(g), rows], AX_X
                                         ).then_inc(psum_ready, 1)
                dve.wait_ge(psum_ready, 2 * g + 2)
                nc.vector.reciprocal(prob_rsum[:, tiles(g)], prob_sum[:, tiles(g)]).then_inc(rsum_ready, 1)

            def x2_half(g):
                dve.wait_ge(rsum_ready, g + 1)
                dve.wait_ge(xbv_out, g + 1)
                dve.wait_ge(av_mm, g + 1)
                for t in range(g * TH, (g + 1) * TH):
                    nc.vector.scalar_tensor_tensor(out=x2[:, t, :], in0=ps_av[g][:, in_half(t)],
                                                   scalar=prob_rsum[:, t:t + 1], in1=x_bv[:, t, :],
                                                   op0=ALU.mult, op1=ALU.add).then_inc(x2_ready, 1)
                for t in range(g * TH, (g + 1) * TH):
                    dve.wait_ge(x2_ready, t + 1)
                    stats_of(1, t, x2)
                for t in range(g * TH, (g + 1) * TH):
                    aggregate(1, t)

            def xn2_half(g):
                dve.wait_ge(rstd_out, G + g + 1)
                for t in range(g * TH, (g + 1) * TH):
                    normalise(1, t, x2, xn2, xn2_ready)

            x2_half(0)
            x2_half(1)
            xn2_half(0)
            xn2_half(1)

            steps = [0]

            def step(ins):
                steps[0] += 1
                ins.then_inc(route_step, 1)
                dve.wait_ge(route_step, steps[0])

            def over_experts(a):
                return a[:, :].unsqueeze(2).to_broadcast([P, NT, E])

            ranks = rank_sb[:, :].unsqueeze(1).to_broadcast([P, NT, E])
            dve.wait_ge(logits_mm, NT)
            step(nc.vector.reduce_max(per_tile["lmax"][:], ps_logits, AX_X))
            nc.vector.tensor_tensor(small["shifted"][:], ps_logits, over_experts(per_tile["lmax"]), ALU.subtract
                                    ).then_inc(route_shift, 1)
            dve.wait_ge(route_exp, 1)
            step(nc.vector.reduce_sum(per_tile["sum"][:], small["exp"][:], AX_X))
            step(nc.vector.reciprocal(per_tile["rsum"][:], per_tile["sum"][:]))
            step(nc.vector.tensor_tensor(small["score"][:], small["exp"][:], over_experts(per_tile["rsum"]), ALU.mult))

            dve.wait_ge(ld["rank"], DMA)

            def largest(src, top, key, hot):
                step(nc.vector.reduce_max(top[:], src[:], AX_X))
                step(nc.vector.tensor_tensor(small["eq"][:], src[:], over_experts(top), ALU.is_equal))
                step(nc.vector.tensor_tensor(small["key"][:], small["eq"][:], ranks, ALU.mult))
                step(nc.vector.reduce_max(key[:], small["key"][:], AX_X))
                step(nc.vector.tensor_tensor(hot[:], small["key"][:], over_experts(key), ALU.is_equal))

            largest(small["score"], per_tile["max1"], per_tile["key1"], small["first"])
            step(nc.vector.scalar_tensor_tensor(out=small["rest"][:], in0=small["first"][:], scalar=-2.0,
                                                in1=small["score"][:], op0=ALU.mult, op1=ALU.add))
            largest(small["rest"], per_tile["max2"], per_tile["key2"], small["second"])
            step(nc.vector.tensor_tensor(small["mask"][:], small["first"][:], small["second"][:], ALU.add))
            step(nc.vector.tensor_tensor(small["masked"][:], small["score"][:], small["mask"][:], ALU.mult))
            dve.wait_ge(zeros_ready, 2)

            def part(p, c):
                return route[:, :, PART_ROWS * p + E * c:PART_ROWS * p + E * (c + 1)]

            step(nc.vector.tensor_copy(part(0, 0), small["masked"][:]))
            step(nc.vector.tensor_tensor(small["r1"][:], small["masked"][:], part(0, 0), ALU.subtract))
            step(nc.vector.tensor_copy(part(1, 0), small["r1"][:]))
            nc.vector.tensor_tensor(part(2, 0), small["r1"][:], part(1, 0), ALU.subtract).then_inc(route_rows, 1)
            nc.vector.tensor_copy(route[:, :, :].rearrange("p t (q c) -> p t q c", c=PART_ROWS)[
                :, :, 0:PARTS, E:2 * E], small["mask"][:, :, :].unsqueeze(2).to_broadcast([P, NT, PARTS, E])
                ).then_inc(route_rows, 1)

            def shared_product(g, c):
                n = C * g + c
                dve.wait_ge(silus, n + 1)
                dve.wait_ge(up_mm, n + 1)
                if g >= 1:
                    dve.wait_ge(a2_mm, g)
                nc.vector.tensor_tensor(gated[:, c, :], gate_act[:, c, :], ps_up(g, c)[:], ALU.mult
                                        ).then_inc(gated_ready, 1)

            def evac_z(g):
                dve.wait_ge(a2_mm, g + 1)
                nc.vector.tensor_copy(z_t[:, tok(g)], ps_z[g][:]).then_inc(prod_out, 1)

            def scale_tokens(s, h):
                dve.wait_ge(bcast_mm, s + 1)
                nc.vector.tensor_tensor(xs[h][:], xn2_t[:, tok(h)], ps_bcast[h][:], ALU.mult).then_inc(xs_out, 1)

            def split_xs(s, h):
                dve.wait_ge(xs_hi_out, s + 1)
                nc.vector.tensor_tensor(xs_lo[h][:], xs[h][:], xs_hi[h][:].bitcast(F32), ALU.subtract
                                        ).then_inc(xs_lo_out, 1)

            shared_product(0, 0)
            shared_product(0, 1)
            evac_z(0)
            shared_product(1, 0)
            shared_product(1, 1)
            dve.wait_ge(xn2t_out, G)
            scale_tokens(0, 0)
            scale_tokens(1, 1)
            split_xs(0, 0)
            evac_z(1)

            def expert_pair(i, last):
                for p in range(2):
                    e = 2 * i + p
                    for h in range(G):
                        s = 4 * i + 2 * p + h
                        if not (last and p == 1 and h == 1):
                            dve.wait_ge(a2_mm, G + s)
                            split_xs(s + 1, 1 - h)
                        if not (last and p == 1):
                            scale_tokens(s + 2, h)
                        if h == 0:
                            dve.wait_ge(ld_w2[p], DMA * (i + 1))
                        dve.wait_ge(a2_mm, G + s + 1)
                        dve.wait_ge(x3_out, s + 1)
                        dve.wait_ge(y_out, s + 1)
                        nc.vector.scalar_tensor_tensor(out=prod[h][:], in0=ps_a2[h][:],
                                                       scalar=w2_sb[p][:, P + 1:P + 2], in1=x3[h][:],
                                                       op0=ALU.add, op1=ALU.mult).then_inc(prod_out, 1)

            with dve.Fori(0, PAIRS - 1) as i:
                expert_pair(i, False)
            expert_pair(PAIRS - 1, True)

        @block.tensor
        def _(pe):
            def mm(out, lhs_t, rhs, start=True, stop=True):
                return nc.tensor.matmul(out, lhs_t, rhs, start=start, stop=stop)

            pe.wait_ge(ld["wk"], DMA)
            for g in range(G):
                pe.wait_ge(ld[f"ctx{g}"], DMA)
                mm(ps_k[g][:], wk_sb[:], ctx_sb[:, tok(g)]).then_inc(kt_mm, 1)
                if g == 0:
                    pe.wait_ge(ld["wv"], DMA)
                for t in range(g * TH, (g + 1) * TH):
                    last = mm(ps_v[g][:, in_half(t)], ctx_sb[:, tile(t)], wv_sb[:])
                last.then_inc(v_mm, 1)
            pe.wait_ge(ld["ident"], DMA)
            pe.wait_ge(ld["wq"], DMA)

            def transposes(g, src, ready, base, dst, done):
                for t in range(g * TH, (g + 1) * TH):
                    pe.wait_ge(ready, base + t + 1)
                    last = nc.tensor.transpose(dst[g][:, in_half(t)], src[:, t, :], ident_sb[:])
                last.then_inc(done, 1)

            for g in range(G):
                transposes(g, xn1, xn1_ready, 0, ps_xn1t, xn1t_mm)
                pe.wait_ge(xn1t_out, g + 1)
                pe.wait_ge(kt_out, g + 1)
                mm(ps_q[g][:], wq_sb[:], xn1_t[:, tok(g)]).then_inc(q_mm, 1)
            for g in range(G):
                pe.wait_ge(q_out, g + 1)
                for t in range(g * TH, (g + 1) * TH):
                    for b in range(2):
                        seq = slice(t * P + b * S, t * P + (b + 1) * S)
                        last = mm(ps_scores[g][b * S:(b + 1) * S, (t % TH) * S:(t % TH + 1) * S],
                                  q_t[:, seq], k_t[:, seq])
                last.then_inc(scores_mm, 1)
            for g in range(G):
                pe.wait_ge(exps, 2 * g + 2)
                for t in range(g * TH, (g + 1) * TH):
                    last = nc.tensor.transpose(ps_pt[g][:, in_half(t)], probs[:, t, :], ident_sb[:])
                last.then_inc(pt_mm, 1)
            for g in range(G):
                pe.wait_ge(pt_out, g + 1)
                pe.wait_ge(v_out, g + 1)
                for t in range(g * TH, (g + 1) * TH):
                    last = mm(ps_av[g][:, in_half(t)], probs_t[:, t, :], v_sb[:, t, :])
                last.then_inc(av_mm, 1)

            def logits(g):
                pe.wait_ge(xn2t_out, g + 1)
                if g == 0:
                    pe.wait_ge(shift_ready, G)
                    pe.wait_ge(ld["gate"], DMA)
                for t in range(g * TH, (g + 1) * TH):
                    mm(ps_logits[:, t, :], xn2_t[:, tile(t)], gate_sb[:]).then_inc(logits_mm, 1)

            def shared_up(g, c):
                mm(ps_gate(g, c)[:], sw12_sb[:, c, :], xn2_t[:, tok(g)]).then_inc(gate_mm, 1)
                mm(ps_up(g, c)[:], sw12_sb[:, C + c, :], xn2_t[:, tok(g)]).then_inc(up_mm, 1)

            def shared_down(g):
                for c in range(C):
                    pe.wait_ge(gated_ready, C * g + c + 1)
                    last = mm(ps_z[g][:], sw3_sb[:, c, :], gated[:, c, :], start=(c == 0), stop=(c == C - 1))
                last.then_inc(a2_mm, 1)

            def broadcast(e, s, h):
                mm(ps_bcast[h][:], pick_score[:, bass.ds(e, 1), :].rearrange("p o d -> p (o d)"),
                   route_t[:, tok(h)]).then_inc(bcast_mm, 1)

            for g in range(G):
                transposes(g, xn2, xn2_ready, 0, ps_xn2t, xn2t_mm)
                transposes(g, x2, x2_ready, 0, ps_x2t, x2t_mm)
            logits(0)
            logits(1)
            pe.wait_ge(ld["sw12"], DMA)
            pe.wait_ge(x2t_out, G)
            shared_up(0, 0)
            shared_up(0, 1)
            pe.wait_ge(ld["sw3"], DMA)
            pe.wait_ge(silus, 2)
            shared_up(1, 0)
            shared_up(1, 1)
            pe.wait_ge(route_rows, 2)
            pe.wait_ge(ident_cast, 1)
            for t in range(NT):
                last = nc.tensor.transpose(ps_route_t[:, tile(t)], route[:, t, :], ident_bf[:])
            last.then_inc(route_mm, 1)
            shared_down(0)
            pe.wait_ge(route_out, 1)
            pe.wait_ge(picks_score, 1)
            pe.wait_ge(silus, 2 * C)
            broadcast(0, 0, 0)
            broadcast(0, 1, 1)
            shared_down(1)
            pe.wait_ge(pick_b3_ready, 1)

            def split_product(out, w, hi, lo, w_lo, stop):
                mm(out, w, hi, start=True, stop=False)
                mm(out, w, lo, start=False, stop=False)
                return mm(out, w_lo, hi, start=False, stop=stop)

            def expert_pair(i, last):
                for p in range(2):
                    e = 2 * i + p
                    for h in range(G):
                        s = 4 * i + 2 * p + h
                        if h == 0:
                            pe.wait_ge(w_lo_out, e + 1)
                        pe.wait_ge(xs_lo_out, s + 1)
                        pe.wait_ge(silus, C * G + s - 1)
                        pe.wait_ge(prod_out, s + 1)
                        split_product(ps_a1[h][:], w13_hi[p][:, 0, :], xs_hi[h][:], xs_lo[h][:], w13_lo[p][:, 0, :],
                                      True).then_inc(a1_mm, 1)
                        if not (last and p == 1):
                            pe.wait_ge(xs_out, s + 1)
                            broadcast(e + 1, s + 2, h)
                        split_product(ps_a3[h][:], w13_hi[p][:, 1, :], xs_hi[h][:], xs_lo[h][:], w13_lo[p][:, 1, :],
                                      False)
                        mm(ps_a3[h][:], pick_b3[:, bass.ds(e, 1), :].rearrange("p o d -> p (o d)"),
                           route_t[:, tok(h)], start=False, stop=True).then_inc(a3_mm, 1)
                        if h == 0:
                            pe.wait_ge(ld_w2[p], DMA * (i + 1))
                        pe.wait_ge(silus, C * G + s + 1)
                        mm(ps_a2[h][:], w2_sb[p][:, 0:P], hidden[h][:]).then_inc(a2_mm, 1)

            with pe.Fori(0, PAIRS - 1) as i:
                expert_pair(i, False)
            expert_pair(PAIRS - 1, True)


def kernel(x, ctx_1024, L0_xattn_Wq, L0_xattn_bq, L0_xattn_Wk, L0_xattn_bk, L0_xattn_Wv, L0_xattn_bv,
           L0_ffn_gate_w, L0_ffn_w1, L0_ffn_b1, L0_ffn_w2, L0_ffn_b2, L0_ffn_w3, L0_ffn_b3,
           L0_ffn_sw1, L0_ffn_sw2, L0_ffn_sw3):
    import numpy as np
    import concourse.bacc as bacc
    from concourse import mybir as _mybir
    from concourse.bass_utils import run_bass_kernel_spmd as run

    a = np.asarray
    batch, seq, d = x.shape
    experts = L0_ffn_w1.shape[0]
    chunks = L0_ffn_sw1.shape[0] // P
    b3_rows = np.zeros((P, d), a(L0_ffn_b3).dtype)
    for p in range(PARTS):
        b3_rows[PART_ROWS * p + experts:PART_ROWS * p + 2 * experts] = a(L0_ffn_b3)
    sw12 = np.concatenate([a(L0_ffn_sw1).reshape(chunks, P, d), a(L0_ffn_sw2).reshape(chunks, P, d)])
    onehots = np.zeros((P, 2 * experts), np.float32)
    for p in range(PARTS):
        for c in range(2 * experts):
            onehots[PART_ROWS * p + c, c] = 1.0
    arrays = {
        "x": a(x).reshape(batch * seq, d),
        "ctx_t": a(ctx_1024).reshape(batch * seq, d).T,
        "wq": a(L0_xattn_Wq), "wk": a(L0_xattn_Wk), "wv": a(L0_xattn_Wv),
        "cols": np.stack([a(L0_xattn_bq), a(L0_xattn_bk)], axis=1),
        "bv": a(L0_xattn_bv),
        "gate_t": a(L0_ffn_gate_w).T,
        "sw12_t": sw12.transpose(2, 0, 1),
        "sw3_t": a(L0_ffn_sw3).T.reshape(chunks, P, d),
        "w13_t": np.stack([a(L0_ffn_w1).transpose(0, 2, 1), a(L0_ffn_w3).transpose(0, 2, 1)], axis=2),
        "w2_t": np.concatenate([a(L0_ffn_w2).transpose(0, 2, 1), a(L0_ffn_b1)[:, :, None], a(L0_ffn_b2)[:, :, None]],
                               axis=2),
        "b3_rows": b3_rows,
        "ident": np.eye(P, dtype=np.float32),
        "onehots": onehots,
        "rank_weight": np.arange(experts, 0, -1).astype(np.float32),
    }
    nc = bacc.Bacc("TRN2", target_bir_lowering=False, num_devices=1)
    feeds, args = {}, []
    for name, value in arrays.items():
        value = np.ascontiguousarray(value)
        feeds[f"in_{name}"] = value
        args.append(nc.dram_tensor(f"in_{name}", value.shape, _mybir.dt.from_np(value.dtype),
                                   kind="ExternalInput").ap())
    args.append(nc.dram_tensor("out_t", (d, batch * seq), _mybir.dt.float32, kind="ExternalOutput").ap())
    xattn_moe_ffn_kernel(nc, *args)
    r = run(nc, [feeds], core_ids=[0])
    return np.ascontiguousarray(r.results[0]["out_t"].T).reshape(batch, seq, d)
```

```python
from contextlib import ExitStack

import concourse.bass as bass
from concourse import mybir

F32 = mybir.dt.float32
F32R = mybir.dt.float32r
BF16 = mybir.dt.bfloat16
ALU = mybir.AluOpType
ACT = mybir.ActivationFunctionType
AX_X = mybir.AxisListType.X

P = 128
EPS = 1e-5
WARM_UP = 9
DMA = 16
PARTS, PART_ROWS = 3, 32


def xattn_moe_ffn_kernel(nc, x, ctx_t, project, value, routing, sw12_t, sw3_t, w13_t, w2_t, out_t):
    T = ctx_t.shape[1]
    NT = T // P
    G = 2
    HALF = T // G
    TH = NT // G
    S = 64
    E = w2_t.shape[0]
    C = sw3_t.shape[0]
    PAIRS = E // 2
    SCALE = 1.0 / float(P) ** 0.5
    assert P == 128 and HALF == 512 and C == 2 and E == 8

    with ExitStack() as ctx:
        def sb(name, shape, dt=F32):
            return ctx.enter_context(nc.sbuf_tensor(name, shape, dt))

        def sem(name):
            return ctx.enter_context(nc.semaphore(name))

        x_sb = sb("x_sb", [P, NT, P])
        ctx_sb = sb("ctx_sb", [P, T])
        project_sb = sb("project_sb", [P, 3 * P + 2])
        wk_sb, ident_sb, wq_sb = (project_sb[:, n * P:(n + 1) * P] for n in range(3))
        bk_sb, bq_sb = (project_sb[:, 3 * P + n:3 * P + n + 1] for n in range(2))
        value_sb = sb("value_sb", [P, 2 * P])
        wv_sb, bv_sb = value_sb[:, 0:P], value_sb[:, P:2 * P]
        routing_sb = sb("routing_sb", [P, P + 4 * E])
        b3_sb = routing_sb[:, 0:P]
        gate_sb = routing_sb[:, P:P + E]
        onehots_sb = routing_sb[:, P + E:P + 3 * E]
        rank_sb = routing_sb[:, P + 3 * E:P + 4 * E]
        sw12_sb = sb("sw12_sb", [P, 2 * C, P])
        sw3_sb = sb("sw3_sb", [P, C, P])
        ident_bf = sb("ident_bf", [P, P], BF16)

        stats = sb("stats", [P, 2, NT, 6])
        mean_var = sb("mean_var", [P, 2, NT, 2])
        var_eps = sb("var_eps", [P, 2, NT])
        rstd = sb("rstd", [P, 2, NT])
        minus_half = sb("minus_half", [P, NT])
        xn1 = sb("xn1", [P, NT, P])
        xn1_t = sb("xn1_t", [P, T])
        q_t, k_t = sb("q_t", [P, T]), sb("k_t", [P, T])
        v_sb = sb("v_sb", [P, NT, P])
        x_bv = sb("x_bv", [P, NT, P])
        score_max = sb("score_max", [P, NT])
        shifted = sb("shifted", [P, NT, S])
        probs = sb("probs", [P, NT, P])
        probs_t = sb("probs_t", [P, NT, P])
        prob_sum = sb("prob_sum", [P, NT])
        prob_rsum = sb("prob_rsum", [P, NT])
        x2 = sb("x2", [P, NT, P])
        xn2 = sb("xn2", [P, NT, P])
        x2_t = sb("x2_t", [P, T])
        xn2_t = sb("xn2_t", [P, T])

        small = {n: sb("route_" + n, [P, NT, E]) for n in (
            "shifted", "exp", "score", "eq", "key", "first", "rest", "second", "mask", "masked", "r1")}
        per_tile = {n: sb("route_" + n, [P, NT]) for n in (
            "lmax", "sum", "rsum", "key1", "max2", "key2")}
        route = sb("route", [P, NT, P], BF16)
        route_t = sb("route_t", [P, T], BF16)
        pick_score = sb("pick_score", [P, E, P], BF16)
        pick_b3 = sb("pick_b3", [P, E, P], BF16)
        b3_part = sb("b3_part", [P, P], BF16)
        b3_q1 = sb("b3_q1", [P, P], BF16)
        b3_r1 = sb("b3_r1", [P, P])
        b3_q2 = sb("b3_q2", [P, P], BF16)
        b3_r2 = sb("b3_r2", [P, P])

        warm = sb("warm", [P, HALF], BF16)
        table_load = sb("table_load", [P, 1])
        gate_act = sb("gate_act", [P, G * C, HALF])
        gated = sb("gated", [P, G * C, HALF])
        z_t = sb("z_t", [P, T])
        y_t = sb("y_t", [P, T])

        w13_raw = [sb(f"w13_raw{p}", [P, 2, P]) for p in range(2)]
        w13_hi = [sb(f"w13_hi{p}", [P, 2, P], F32R) for p in range(2)]
        w13_lo = [sb(f"w13_lo{p}", [P, 2, P], F32R) for p in range(2)]
        w2_sb = [sb(f"w2_sb{p}", [P, P + 2]) for p in range(2)]
        xs = [sb(f"xs{h}", [P, HALF]) for h in range(G)]
        xs_hi = [sb(f"xs_hi{h}", [P, HALF], F32R) for h in range(G)]
        xs_lo = [sb(f"xs_lo{h}", [P, HALF], F32R) for h in range(G)]
        hidden = [sb(f"hidden{h}", [P, HALF]) for h in range(G)]
        x3 = [sb(f"x3{h}", [P, HALF]) for h in range(G)]
        prod = [sb(f"prod{h}", [P, HALF]) for h in range(G)]

        bank = [ctx.enter_context(nc.psum_tensor(f"bank{i}", [P, 512], F32)) for i in range(8)]
        ps_k = ps_q = ps_x2t = ps_z = ps_a1 = [bank[0], bank[1]]
        ps_v = ps_av = ps_a3 = [bank[2], bank[3]]
        ps_xn1t = ps_pt = ps_xn2t = ps_a2 = [bank[4], bank[5]]
        ps_scores = ps_bcast = [bank[6], bank[7]]
        ps_logits = bank[7][:, 0:NT * E].rearrange("p (t e) -> p t e", e=E)
        ps_route_t = bank[7][:, :].bitcast(BF16)
        ps_gate = lambda g, c: bank[g] if c == 0 else bank[6 + g]
        ps_up = lambda g, c: bank[2 + g] if c == 0 else bank[4 + g]

        ld = {n: sem("ld_" + n) for n in (
            "x0", "x1", "ctx0", "ctx1", "project", "value", "routing", "sw12", "sw3")}
        ld_w13 = [sem(f"ld_w13_{p}") for p in range(2)]
        ld_w2 = [sem(f"ld_w2_{p}") for p in range(2)]
        stored = sem("stored")
        y_last = [sem(f"y_last{h}") for h in range(G)]
        (kt_mm, v_mm, xn1t_mm, q_mm, scores_mm, pt_mm, av_mm, x2t_mm, xn2t_mm, logits_mm,
         gate_mm, up_mm, route_mm, bcast_mm, a1_mm, a3_mm, a2_mm) = (sem(n) for n in (
            "kt_mm", "v_mm", "xn1t_mm", "q_mm", "scores_mm", "pt_mm", "av_mm", "x2t_mm", "xn2t_mm", "logits_mm",
            "gate_mm", "up_mm", "route_mm", "bcast_mm", "a1_mm", "a3_mm", "a2_mm"))
        (kt_out, v_out, xn1t_out, q_out, exps, pt_out, x2t_out, xn2t_out, route_exp, silus,
         route_out, x3_out, xs_hi_out, w_hi_out, picks_score, ident_cast) = (sem(n) for n in (
            "kt_out", "v_out", "xn1t_out", "q_out", "exps", "pt_out", "x2t_out", "xn2t_out", "route_exp", "silus",
            "route_out", "x3_out", "xs_hi_out", "w_hi_out", "picks_score", "ident_cast"))
        (stat_dve, var_ready, xn1_ready, smax_ready, shift_ready, psum_ready, rsum_ready, x2_ready, xn2_ready,
         route_step, route_shift, route_rows, gated_ready, xs_out, xs_lo_out, prod_out) = (sem(n) for n in (
            "stat_dve", "var_ready", "xn1_ready", "smax_ready", "shift_ready", "psum_ready", "rsum_ready", "x2_ready",
            "xn2_ready", "route_step", "route_shift", "route_rows", "gated_ready", "xs_out", "xs_lo_out", "prod_out"))
        (warm_ready, table_loaded, consts_ready, zeros_ready, var_eps_out, rstd_out, xbv_out, b3_step, pick_b3_ready, w_lo_out, y_out) = (
            sem(n) for n in (
                "warm_ready", "table_loaded", "consts_ready", "zeros_ready", "var_eps_out", "rstd_out", "xbv_out", "b3_step", "pick_b3_ready",
                "w_lo_out", "y_out"))

        tok = lambda g: slice(g * HALF, (g + 1) * HALF)
        tile = lambda t: slice(t * P, (t + 1) * P)
        tiles = lambda g: slice(g * TH, (g + 1) * TH)
        in_half = lambda t: slice((t % TH) * P, (t % TH + 1) * P)

        x_rows = x.rearrange("(t p) d -> p t d", p=P)

        block = ctx.enter_context(nc.Block())

        @block.sync
        def _(sp):
            sp.dma_start(x_sb[:, tiles(0), :], x_rows[:, tiles(0), :]).then_inc(ld["x0"], DMA)
            sp.dma_start(project_sb[:], project).then_inc(ld["project"], DMA)
            sp.dma_start(ctx_sb[:, tok(0)], ctx_t[:, tok(0)]).then_inc(ld["ctx0"], DMA)
            sp.dma_start(x_sb[:, tiles(1), :], x_rows[:, tiles(1), :]).then_inc(ld["x1"], DMA)
            sp.dma_start(value_sb[:], value).then_inc(ld["value"], DMA)
            sp.dma_start(ctx_sb[:, tok(1)], ctx_t[:, tok(1)]).then_inc(ld["ctx1"], DMA)
            sp.dma_start(routing_sb[:], routing).then_inc(ld["routing"], DMA)
            sp.dma_start(sw12_sb[:], sw12_t).then_inc(ld["sw12"], DMA)
            sp.dma_start(sw3_sb[:], sw3_t.rearrange("c h d -> h c d")).then_inc(ld["sw3"], DMA)
            for p in range(2):
                sp.dma_start(w13_raw[p][:], w13_t[p]).then_inc(ld_w13[p], DMA)
                sp.dma_start(w2_sb[p][:], w2_t[p]).then_inc(ld_w2[p], DMA)
            with sp.Fori(0, PAIRS - 1) as i:
                for p in range(2):
                    sp.wait_ge(w_lo_out, 2 * i + p + 1)
                    sp.dma_start(w13_raw[p][:], w13_t[bass.ds(2 * i + p + 2, 1)].rearrange("o d c h -> (o d) c h")
                                 ).then_inc(ld_w13[p], DMA)
                    sp.wait_ge(prod_out, G + 4 * i + 2 * p + 2)
                    sp.dma_start(w2_sb[p][:], w2_t[bass.ds(2 * i + p + 2, 1)].rearrange("o h d -> (o h) d")
                                 ).then_inc(ld_w2[p], DMA)
            for h in range(G):
                sp.wait_ge(y_last[h], 1)
                sp.dma_start(out_t[:, tok(h)], y_t[:, tok(h)]).then_inc(stored, DMA)
            sp.wait_ge(stored, DMA * G)

        @block.gpsimd
        def _(pool):
            nc.gpsimd.memset(minus_half[:], -0.5).then_inc(consts_ready, 1)
            nc.gpsimd.memset(probs[:], 0.0).then_inc(zeros_ready, 1)
            nc.gpsimd.memset(route[:], 0.0).then_inc(zeros_ready, 1)

            def rsqrt_var(norm, g):
                pool.wait_ge(var_ready, G * norm + g + 1)
                nc.gpsimd.tensor_scalar(var_eps[:, norm, tiles(g)], mean_var[:, norm, tiles(g), 1], EPS, None,
                                        ALU.add).then_inc(var_eps_out, 1)
                pool.wait_ge(var_eps_out, G * norm + g + 1)
                pool.wait_ge(consts_ready, 1)
                nc.gpsimd.tensor_tensor(rstd[:, norm, tiles(g)], var_eps[:, norm, tiles(g)], minus_half[:, tiles(g)],
                                        ALU.pow).then_inc(rstd_out, 1)

            rsqrt_var(0, 0)
            rsqrt_var(0, 1)
            pool.wait_ge(ld["value"], DMA)
            for g in range(G):
                pool.wait_ge(ld[f"x{g}"], DMA)
                nc.gpsimd.tensor_tensor(x_bv[:, tiles(g), :], x_sb[:, tiles(g), :],
                                        bv_sb.unsqueeze(1).to_broadcast([P, TH, P]), ALU.add
                                        ).then_inc(xbv_out, 1)
            pool.wait_ge(ld["routing"], DMA)
            nc.gpsimd.tensor_copy(b3_q1[:], b3_sb).then_inc(b3_step, 1)
            pool.wait_ge(b3_step, 1)
            nc.gpsimd.tensor_tensor(b3_r1[:], b3_sb, b3_q1[:], ALU.subtract).then_inc(b3_step, 1)
            pool.wait_ge(b3_step, 2)
            nc.gpsimd.tensor_copy(b3_q2[:], b3_r1[:]).then_inc(b3_step, 1)
            pool.wait_ge(b3_step, 3)
            nc.gpsimd.tensor_tensor(b3_r2[:], b3_r1[:], b3_q2[:], ALU.subtract).then_inc(b3_step, 1)
            pool.wait_ge(b3_step, 4)
            nc.gpsimd.tensor_copy(b3_part[:], b3_r2[:]).then_inc(b3_step, 1)
            pool.wait_ge(b3_step, 5)
            nc.gpsimd.tensor_copy(b3_part[0:PART_ROWS, :], b3_q1[0:PART_ROWS, :]).then_inc(b3_step, 1)
            nc.gpsimd.tensor_copy(b3_part[PART_ROWS:2 * PART_ROWS, :], b3_q2[PART_ROWS:2 * PART_ROWS, :]
                                  ).then_inc(b3_step, 1)
            pool.wait_ge(b3_step, 7)
            nc.gpsimd.tensor_tensor(pick_b3[:], b3_part[:, :].unsqueeze(1).to_broadcast([P, E, P]),
                                    onehots_sb[:, E:2 * E].unsqueeze(2).to_broadcast([P, E, P]), ALU.mult
                                    ).then_inc(pick_b3_ready, 1)
            rsqrt_var(1, 0)
            rsqrt_var(1, 1)

            def split_low(e, p, i):
                pool.wait_ge(w_hi_out, e + 1)
                nc.gpsimd.tensor_tensor(w13_lo[p][:], w13_raw[p][:], w13_hi[p][:].bitcast(F32), ALU.subtract
                                        ).then_inc(w_lo_out, 1)

            split_low(0, 0, 0)
            for g in range(G):
                pool.wait_ge(prod_out, g + 1)
                pool.wait_ge(x2t_out, g + 1)
                nc.gpsimd.tensor_tensor(y_t[:, tok(g)], x2_t[:, tok(g)], z_t[:, tok(g)], ALU.add).then_inc(y_out, 1)

            def add_pair(i, last):
                for p in range(2):
                    for h in range(G):
                        s = 4 * i + 2 * p + h
                        if h == 0 and not (last and p == 1):
                            split_low(2 * i + p + 1, 1 - p, i)
                        if last and p == 1:
                            continue
                        pool.wait_ge(prod_out, G + s + 1)
                        pool.wait_ge(y_out, s + 1)
                        nc.gpsimd.tensor_tensor(y_t[:, tok(h)], y_t[:, tok(h)], prod[h][:], ALU.add
                                                ).then_inc(y_out, 1)

            with pool.Fori(0, PAIRS - 1) as i:
                add_pair(i, False)
            add_pair(PAIRS - 1, True)

        @block.scalar
        def _(act):
            act.wait_ge(ld["project"], DMA)
            nc.scalar.activation(ident_bf[:], ident_sb, ACT.Copy).then_inc(ident_cast, 1)

            def evac_k(g):
                act.wait_ge(kt_mm, g + 1)
                nc.scalar.activation(k_t[:, tok(g)], ps_k[g][:], ACT.Identity, bias=bk_sb
                                     ).then_inc(kt_out, 1)

            def evac_v(g):
                act.wait_ge(v_mm, g + 1)
                nc.scalar.activation(v_sb[:, tiles(g), :], ps_v[g][:].rearrange("p (t d) -> p t d", d=P), ACT.Copy
                                     ).then_inc(v_out, 1)

            def evac_xn1t(g):
                act.wait_ge(xn1t_mm, g + 1)
                nc.scalar.activation(xn1_t[:, tok(g)], ps_xn1t[g][:], ACT.Copy).then_inc(xn1t_out, 1)

            def evac_q(g):
                act.wait_ge(q_mm, g + 1)
                nc.scalar.activation(q_t[:, tok(g)], ps_q[g][:], ACT.Identity, bias=bq_sb
                                     ).then_inc(q_out, 1)

            def exp_scores(g):
                act.wait_ge(shift_ready, g + 1)
                for b in range(2):
                    rows = slice(b * S, (b + 1) * S)
                    nc.scalar.activation(probs[rows, tiles(g), rows], shifted[rows, tiles(g), :], ACT.Exp,
                                         scale=SCALE).then_inc(exps, 1)

            def evac_pt(g):
                act.wait_ge(pt_mm, g + 1)
                nc.scalar.activation(probs_t[:, tiles(g), :], ps_pt[g][:].rearrange("p (t d) -> p t d", d=P), ACT.Copy
                                     ).then_inc(pt_out, 1)

            def evac_xn2t(g):
                act.wait_ge(xn2t_mm, g + 1)
                nc.scalar.activation(xn2_t[:, tok(g)], ps_xn2t[g][:], ACT.Copy).then_inc(xn2t_out, 1)

            def evac_x2t(g):
                act.wait_ge(x2t_mm, g + 1)
                nc.scalar.activation(x2_t[:, tok(g)], ps_x2t[g][:], ACT.Copy).then_inc(x2t_out, 1)

            evac_k(0)
            evac_xn1t(0)
            evac_q(0)
            evac_k(1)
            evac_v(0)
            evac_xn1t(1)
            act.wait_ge(zeros_ready, 1)
            exp_scores(0)
            evac_q(1)
            evac_pt(0)
            evac_v(1)
            exp_scores(1)
            evac_pt(1)
            act.wait_ge(ld["routing"], DMA)
            nc.scalar.activation(pick_score[:], onehots_sb[:, 0:E].unsqueeze(2).to_broadcast([P, E, P]), ACT.Copy
                                 ).then_inc(picks_score, 1)
            def shared_silu(g, c):
                act.wait_ge(gate_mm, C * g + c + 1)
                nc.scalar.activation(gate_act[:, C * g + c, :], ps_gate(g, c)[:], ACT.Silu).then_inc(silus, 1)

            evac_x2t(0)
            evac_xn2t(0)
            shared_silu(0, 0)
            evac_x2t(1)
            shared_silu(0, 1)
            evac_xn2t(1)
            nc.scalar.activation(table_load[:], ident_bf[:, 0:1], ACT.Exp).then_inc(table_loaded, 1)
            act.wait_ge(route_shift, 1)
            nc.scalar.activation(small["exp"][:], small["shifted"][:], ACT.Exp).then_inc(route_exp, 1)

            def split_high(e, p, loads):
                act.wait_ge(ld_w13[p], loads)
                nc.scalar.activation(w13_hi[p][:], w13_raw[p][:], ACT.Copy).then_inc(w_hi_out, 1)

            for c in range(C):
                shared_silu(1, c)
            split_high(0, 0, DMA)
            act.wait_ge(route_mm, 1)
            for g in range(G):
                nc.scalar.activation(route_t[:, tok(g)], ps_route_t[:, tok(g)], ACT.Copy).then_inc(route_out, 1)

            def round_xs(s, h):
                act.wait_ge(xs_out, s + 1)
                nc.scalar.activation(xs_hi[h][:], xs[h][:], ACT.Copy).then_inc(xs_hi_out, 1)

            round_xs(0, 0)
            round_xs(1, 1)

            def expert_pair(i, last):
                for p in range(2):
                    e = 2 * i + p
                    for h in range(G):
                        s = 4 * i + 2 * p + h
                        if h == 0 and not (last and p == 1):
                            act.wait_ge(a2_mm, G + 2 * e)
                            split_high(e + 1, 1 - p, DMA * (i + 1 + p))
                        if h == 0:
                            act.wait_ge(ld_w2[p], DMA * (i + 1))
                        act.wait_ge(a1_mm, s + 1)
                        act.wait_ge(a2_mm, s + 1)
                        nc.scalar.activation(hidden[h][:], ps_a1[h][:], ACT.Silu,
                                             bias=w2_sb[p][:, P:P + 1]).then_inc(silus, 1)
                        act.wait_ge(a3_mm, s + 1)
                        act.wait_ge(prod_out, s + 1)
                        nc.scalar.activation(x3[h][:], ps_a3[h][:], ACT.Copy).then_inc(x3_out, 1)
                        if not (last and p == 1):
                            round_xs(s + 2, h)

            with act.Fori(0, PAIRS - 1) as i:
                expert_pair(i, False)
            expert_pair(PAIRS - 1, True)

        @block.vector
        def _(dve):
            def stats_of(norm, t, src):
                nc.vector.bn_stats(stats[:, norm, t, :], src[:, t, :]).then_inc(stat_dve, 1)

            def aggregate(norm, t):
                dve.wait_ge(stat_dve, norm * NT + t + 1)
                ins = nc.vector.bn_aggr(mean_var[:, norm, t, :], stats[:, norm, t, :])
                if t % TH == TH - 1:
                    ins.then_inc(var_ready, 1)

            def normalise(norm, t, src, dst, ready):
                nc.vector.tensor_scalar(dst[:, t, :], src[:, t, :], mean_var[:, norm, t, 0:1],
                                        rstd[:, norm, t:t + 1], ALU.subtract, ALU.mult).then_inc(ready, 1)

            nc.vector.memset(warm[:], 0.0).then_inc(warm_ready, 1)

            for g in range(G):
                dve.wait_ge(ld[f"x{g}"], DMA)
                for t in range(g * TH, (g + 1) * TH):
                    stats_of(0, t, x_sb)
                for t in range(g * TH, (g + 1) * TH):
                    aggregate(0, t)
            for g in range(G):
                dve.wait_ge(rstd_out, g + 1)
                for t in range(g * TH, (g + 1) * TH):
                    normalise(0, t, x_sb, xn1, xn1_ready)

            def shift_scores(g):
                scores = ps_scores[g][:, 0:TH * S].rearrange("p (t k) -> p t k", k=S)
                dve.wait_ge(scores_mm, g + 1)
                nc.vector.reduce_max(score_max[:, tiles(g)], scores, AX_X).then_inc(smax_ready, 1)
                dve.wait_ge(smax_ready, g + 1)
                nc.vector.tensor_tensor(shifted[:, tiles(g), :], scores,
                                        score_max[:, tiles(g)].unsqueeze(2).to_broadcast([P, TH, S]),
                                        ALU.subtract).then_inc(shift_ready, 1)

            def sum_probs(g):
                for b in range(2):
                    rows = slice(b * S, (b + 1) * S)
                    dve.wait_ge(exps, 2 * g + b + 1)
                    nc.vector.reduce_sum(prob_sum[rows, tiles(g)], probs[rows, tiles(g), rows], AX_X
                                         ).then_inc(psum_ready, 1)
                dve.wait_ge(psum_ready, 2 * g + 2)
                nc.vector.reciprocal(prob_rsum[:, tiles(g)], prob_sum[:, tiles(g)]).then_inc(rsum_ready, 1)

            def x2_half(g):
                dve.wait_ge(rsum_ready, g + 1)
                dve.wait_ge(xbv_out, g + 1)
                dve.wait_ge(av_mm, g + 1)
                for t in range(g * TH, (g + 1) * TH):
                    nc.vector.scalar_tensor_tensor(out=x2[:, t, :], in0=ps_av[g][:, in_half(t)],
                                                   scalar=prob_rsum[:, t:t + 1], in1=x_bv[:, t, :],
                                                   op0=ALU.mult, op1=ALU.add).then_inc(x2_ready, 1)
                for t in range(g * TH, (g + 1) * TH):
                    dve.wait_ge(x2_ready, t + 1)
                    stats_of(1, t, x2)
                for t in range(g * TH, (g + 1) * TH):
                    aggregate(1, t)

            def xn2_half(g):
                dve.wait_ge(rstd_out, G + g + 1)
                for t in range(g * TH, (g + 1) * TH):
                    normalise(1, t, x2, xn2, xn2_ready)

            shift_scores(0)
            sum_probs(0)
            shift_scores(1)
            x2_half(0)
            sum_probs(1)
            xn2_half(0)
            x2_half(1)
            xn2_half(1)

            def shared_product(g, c):
                n = C * g + c
                dve.wait_ge(silus, n + 1)
                dve.wait_ge(up_mm, n + 1)
                nc.vector.tensor_tensor(gated[:, n, :], gate_act[:, n, :], ps_up(g, c)[:], ALU.mult
                                        ).then_inc(gated_ready, 1)

            steps = [0]

            def step(ins):
                steps[0] += 1
                ins.then_inc(route_step, 1)
                return steps[0]

            def after(n):
                dve.wait_ge(route_step, n)

            def over_experts(a):
                return a[:, :].unsqueeze(2).to_broadcast([P, NT, E])

            def first_of_equals(key, hot, eq_done, fill=()):
                after(eq_done)
                n = step(nc.vector.tensor_tensor(small["key"][:], small["eq"][:], ranks, ALU.mult))
                after(n)
                n = step(nc.vector.reduce_max(key[:], small["key"][:], AX_X))
                after(n)
                return step(nc.vector.tensor_tensor(hot[:], small["key"][:], over_experts(key), ALU.is_equal))

            shared_product(0, 0)
            shared_product(0, 1)
            ranks = rank_sb.unsqueeze(1).to_broadcast([P, NT, E])
            dve.wait_ge(ld["routing"], DMA)
            dve.wait_ge(logits_mm, NT)
            n = step(nc.vector.reduce_max(per_tile["lmax"][:], ps_logits, AX_X))
            after(n)
            nc.vector.tensor_tensor(small["shifted"][:], ps_logits, over_experts(per_tile["lmax"]), ALU.subtract
                                    ).then_inc(route_shift, 1)
            logits_read = step(nc.vector.tensor_tensor(small["eq"][:], ps_logits, over_experts(per_tile["lmax"]),
                                                       ALU.is_equal))
            first = first_of_equals(per_tile["key1"], small["first"], logits_read)
            dve.wait_ge(route_exp, 1)
            after(first)
            rest = step(nc.vector.scalar_tensor_tensor(out=small["rest"][:], in0=small["first"][:], scalar=-2.0,
                                                       in1=small["exp"][:], op0=ALU.mult, op1=ALU.add))
            total = step(nc.vector.reduce_sum(per_tile["sum"][:], small["exp"][:], AX_X))
            after(rest)
            top = step(nc.vector.reduce_max(per_tile["max2"][:], small["rest"][:], AX_X))
            after(total)
            inverse = step(nc.vector.reciprocal(per_tile["rsum"][:], per_tile["sum"][:]))
            after(top)
            equal = step(nc.vector.tensor_tensor(small["eq"][:], small["rest"][:], over_experts(per_tile["max2"]),
                                                 ALU.is_equal))
            after(inverse)
            step(nc.vector.tensor_tensor(small["score"][:], small["exp"][:], over_experts(per_tile["rsum"]), ALU.mult))
            second = first_of_equals(per_tile["key2"], small["second"], equal)
            after(second)
            n = step(nc.vector.tensor_tensor(small["mask"][:], small["first"][:], small["second"][:], ALU.add))
            after(n)
            dve.wait_ge(zeros_ready, 2)

            def part(p, c):
                return route[:, :, PART_ROWS * p + E * c:PART_ROWS * p + E * (c + 1)]

            step(nc.vector.tensor_tensor(small["masked"][:], small["score"][:], small["mask"][:], ALU.mult))
            n = step(nc.vector.tensor_tensor(part(0, 0), small["score"][:], small["mask"][:], ALU.mult))
            after(n)
            step(nc.vector.tensor_tensor(small["r1"][:], small["masked"][:], part(0, 0), ALU.subtract))
            n = step(nc.vector.tensor_tensor(part(1, 0), small["masked"][:], part(0, 0), ALU.subtract))
            nc.vector.tensor_copy(route[:, :, :].rearrange("p t (q c) -> p t q c", c=PART_ROWS)[
                :, :, 0:PARTS, E:2 * E], small["mask"][:, :, :].unsqueeze(2).to_broadcast([P, NT, PARTS, E])
                ).then_inc(route_rows, 1)
            after(n)
            nc.vector.tensor_tensor(part(2, 0), small["r1"][:], part(1, 0), ALU.subtract).then_inc(route_rows, 1)

            def evac_z(g):
                dve.wait_ge(a2_mm, g + 1)
                nc.vector.tensor_copy(z_t[:, tok(g)], ps_z[g][:]).then_inc(prod_out, 1)

            def scale_tokens(s, h):
                dve.wait_ge(bcast_mm, s + 1)
                nc.vector.tensor_tensor(xs[h][:], xn2_t[:, tok(h)], ps_bcast[h][:], ALU.mult).then_inc(xs_out, 1)

            def split_xs(s, h):
                dve.wait_ge(xs_hi_out, s + 1)
                nc.vector.tensor_tensor(xs_lo[h][:], xs[h][:], xs_hi[h][:].bitcast(F32), ALU.subtract
                                        ).then_inc(xs_lo_out, 1)

            shared_product(1, 0)
            shared_product(1, 1)
            dve.wait_ge(xn2t_out, G)
            scale_tokens(0, 0)
            evac_z(0)
            split_xs(0, 0)
            scale_tokens(1, 1)
            evac_z(1)

            def expert_pair(i, last):
                for p in range(2):
                    e = 2 * i + p
                    for h in range(G):
                        s = 4 * i + 2 * p + h
                        if not (last and p == 1 and h == 1):
                            dve.wait_ge(a2_mm, G + s)
                            split_xs(s + 1, 1 - h)
                        if not (last and p == 1):
                            scale_tokens(s + 2, h)
                        if h == 0:
                            dve.wait_ge(ld_w2[p], DMA * (i + 1))
                        dve.wait_ge(a2_mm, G + s + 1)
                        dve.wait_ge(x3_out, s + 1)
                        dve.wait_ge(y_out, s + 1)
                        nc.vector.scalar_tensor_tensor(out=prod[h][:], in0=ps_a2[h][:],
                                                       scalar=w2_sb[p][:, P + 1:P + 2], in1=x3[h][:],
                                                       op0=ALU.add, op1=ALU.mult).then_inc(prod_out, 1)
                        if last and p == 1:
                            dve.wait_ge(prod_out, G + s + 1)
                            dve.wait_ge(y_out, G + s - 1)
                            nc.vector.tensor_tensor(y_t[:, tok(h)], y_t[:, tok(h)], prod[h][:], ALU.add
                                                    ).then_inc(y_last[h], 1)

            with dve.Fori(0, PAIRS - 1) as i:
                expert_pair(i, False)
            expert_pair(PAIRS - 1, True)

        @block.tensor
        def _(pe):
            def mm(out, lhs_t, rhs, start=True, stop=True):
                return nc.tensor.matmul(out, lhs_t, rhs, start=start, stop=stop)

            def keys(g):
                pe.wait_ge(ld["project"], DMA)
                pe.wait_ge(ld[f"ctx{g}"], DMA)
                mm(ps_k[g][:], wk_sb, ctx_sb[:, tok(g)]).then_inc(kt_mm, 1)

            def values(g, first, end):
                pe.wait_ge(ld["value"], DMA)
                pe.wait_ge(ld[f"ctx{g}"], DMA)
                for t in range(g * TH + first, g * TH + end):
                    last = mm(ps_v[g][:, in_half(t)], ctx_sb[:, tile(t)], wv_sb)
                if end == TH:
                    last.then_inc(v_mm, 1)

            def transposes(g, src, ready, dst, done):
                for t in range(g * TH, (g + 1) * TH):
                    pe.wait_ge(ready, t + 1)
                    last = nc.tensor.transpose(dst[g][:, in_half(t)], src[:, t, :], ident_sb)
                last.then_inc(done, 1)

            def queries(g):
                pe.wait_ge(xn1t_out, g + 1)
                pe.wait_ge(kt_out, g + 1)
                mm(ps_q[g][:], wq_sb, xn1_t[:, tok(g)]).then_inc(q_mm, 1)

            def scores(g):
                pe.wait_ge(q_out, g + 1)
                for t in range(g * TH, (g + 1) * TH):
                    for b in range(2):
                        seq = slice(t * P + b * S, t * P + (b + 1) * S)
                        last = mm(ps_scores[g][b * S:(b + 1) * S, (t % TH) * S:(t % TH + 1) * S],
                                  q_t[:, seq], k_t[:, seq])
                last.then_inc(scores_mm, 1)

            def turn_probs(g):
                pe.wait_ge(exps, 2 * g + 2)
                for t in range(g * TH, (g + 1) * TH):
                    last = nc.tensor.transpose(ps_pt[g][:, in_half(t)], probs[:, t, :], ident_sb)
                last.then_inc(pt_mm, 1)

            def attend(g):
                pe.wait_ge(pt_out, g + 1)
                pe.wait_ge(v_out, g + 1)
                for t in range(g * TH, (g + 1) * TH):
                    last = mm(ps_av[g][:, in_half(t)], probs_t[:, t, :], v_sb[:, t, :])
                last.then_inc(av_mm, 1)

            def logits(g):
                pe.wait_ge(xn2t_out, g + 1)
                if g == 0:
                    pe.wait_ge(ld["routing"], DMA)
                for t in range(g * TH, (g + 1) * TH):
                    mm(ps_logits[:, t, :], xn2_t[:, tile(t)], gate_sb).then_inc(logits_mm, 1)

            def shared_gate(g, c):
                mm(ps_gate(g, c)[:], sw12_sb[:, c, :], xn2_t[:, tok(g)]).then_inc(gate_mm, 1)

            def shared_up(g, c):
                mm(ps_up(g, c)[:], sw12_sb[:, C + c, :], xn2_t[:, tok(g)]).then_inc(up_mm, 1)

            def shared_down(g):
                for c in range(C):
                    pe.wait_ge(gated_ready, C * g + c + 1)
                    last = mm(ps_z[g][:], sw3_sb[:, c, :], gated[:, C * g + c, :], start=(c == 0), stop=(c == C - 1))
                last.then_inc(a2_mm, 1)

            def broadcast(e, s, h):
                mm(ps_bcast[h][:], pick_score[:, bass.ds(e, 1), :].rearrange("p o d -> p (o d)"),
                   route_t[:, tok(h)]).then_inc(bcast_mm, 1)

            def stay_warm(times, b):
                for _ in range(times):
                    mm(bank[b][:], warm[:, 0:P], warm[:])

            pe.wait_ge(warm_ready, 1)
            stay_warm(WARM_UP, 7)
            keys(0)
            transposes(0, xn1, xn1_ready, ps_xn1t, xn1t_mm)
            values(0, 0, TH - 1)
            queries(0)
            keys(1)
            scores(0)
            values(0, TH - 1, TH)
            transposes(1, xn1, xn1_ready, ps_xn1t, xn1t_mm)
            queries(1)
            turn_probs(0)
            values(1, 0, TH)
            scores(1)
            attend(0)
            turn_probs(1)
            attend(1)
            transposes(0, x2, x2_ready, ps_x2t, x2t_mm)
            transposes(0, xn2, xn2_ready, ps_xn2t, xn2t_mm)
            pe.wait_ge(shift_ready, G)
            stay_warm(4, 6)
            pe.wait_ge(xn2t_out, 1)
            pe.wait_ge(ld["sw12"], DMA)
            pe.wait_ge(x2t_out, 1)
            shared_gate(0, 0)
            shared_gate(0, 1)
            transposes(1, x2, x2_ready, ps_x2t, x2t_mm)
            shared_up(0, 0)
            logits(0)
            transposes(1, xn2, xn2_ready, ps_xn2t, xn2t_mm)
            shared_up(0, 1)
            logits(1)
            pe.wait_ge(x2t_out, 2)
            shared_gate(1, 0)
            pe.wait_ge(route_step, 2)
            shared_gate(1, 1)
            shared_up(1, 0)
            shared_up(1, 1)
            pe.wait_ge(ld["sw3"], DMA)
            shared_down(0)
            pe.wait_ge(route_rows, 2)
            pe.wait_ge(ident_cast, 1)
            pe.wait_ge(silus, G * C)
            for t in range(NT):
                last = nc.tensor.transpose(ps_route_t[:, tile(t)], route[:, t, :], ident_bf[:])
            last.then_inc(route_mm, 1)
            pe.wait_ge(picks_score, 1)
            pe.wait_ge(route_out, 1)
            broadcast(0, 0, 0)
            pe.wait_ge(route_out, 2)
            broadcast(0, 1, 1)
            shared_down(1)
            pe.wait_ge(pick_b3_ready, 1)

            def split_product(out, w, hi, lo, w_lo, stop):
                mm(out, w, hi, start=True, stop=False)
                mm(out, w, lo, start=False, stop=False)
                return mm(out, w_lo, hi, start=False, stop=stop)

            def expert_pair(i, last):
                for p in range(2):
                    e = 2 * i + p
                    for h in range(G):
                        s = 4 * i + 2 * p + h
                        if h == 0:
                            pe.wait_ge(w_lo_out, e + 1)
                        pe.wait_ge(xs_lo_out, s + 1)
                        pe.wait_ge(silus, C * G + s - 1)
                        pe.wait_ge(prod_out, s + 1)
                        split_product(ps_a1[h][:], w13_hi[p][:, 0, :], xs_hi[h][:], xs_lo[h][:], w13_lo[p][:, 0, :],
                                      True).then_inc(a1_mm, 1)
                        if not (last and p == 1):
                            pe.wait_ge(xs_out, s + 1)
                            broadcast(e + 1, s + 2, h)
                        split_product(ps_a3[h][:], w13_hi[p][:, 1, :], xs_hi[h][:], xs_lo[h][:], w13_lo[p][:, 1, :],
                                      False)
                        mm(ps_a3[h][:], pick_b3[:, bass.ds(e, 1), :].rearrange("p o d -> p (o d)"),
                           route_t[:, tok(h)], start=False, stop=True).then_inc(a3_mm, 1)
                        if h == 0:
                            pe.wait_ge(ld_w2[p], DMA * (i + 1))
                        pe.wait_ge(silus, C * G + s + 1)
                        mm(ps_a2[h][:], w2_sb[p][:, 0:P], hidden[h][:]).then_inc(a2_mm, 1)

            with pe.Fori(0, PAIRS - 1) as i:
                expert_pair(i, False)
            expert_pair(PAIRS - 1, True)


def kernel(x, ctx_1024, L0_xattn_Wq, L0_xattn_bq, L0_xattn_Wk, L0_xattn_bk, L0_xattn_Wv, L0_xattn_bv,
           L0_ffn_gate_w, L0_ffn_w1, L0_ffn_b1, L0_ffn_w2, L0_ffn_b2, L0_ffn_w3, L0_ffn_b3,
           L0_ffn_sw1, L0_ffn_sw2, L0_ffn_sw3):
    import numpy as np
    import concourse.bacc as bacc
    from concourse import mybir as _mybir
    from concourse.bass_utils import run_bass_kernel_spmd as run

    a = np.asarray
    batch, seq, d = x.shape
    experts = L0_ffn_w1.shape[0]
    chunks = L0_ffn_sw1.shape[0] // P
    b3_rows = np.zeros((P, d), a(L0_ffn_b3).dtype)
    for p in range(PARTS):
        b3_rows[PART_ROWS * p + experts:PART_ROWS * p + 2 * experts] = a(L0_ffn_b3)
    sw12 = np.concatenate([a(L0_ffn_sw1).reshape(chunks, P, d), a(L0_ffn_sw2).reshape(chunks, P, d)])
    onehots = np.zeros((P, 2 * experts), np.float32)
    for p in range(PARTS):
        for c in range(2 * experts):
            onehots[PART_ROWS * p + c, c] = 1.0
    arrays = {
        "x": a(x).reshape(batch * seq, d),
        "ctx_t": a(ctx_1024).reshape(batch * seq, d).T,
        "project": np.concatenate([a(L0_xattn_Wk), np.eye(P, dtype=np.float32), a(L0_xattn_Wq),
                                   a(L0_xattn_bk)[:, None], a(L0_xattn_bq)[:, None]], axis=1),
        "value": np.concatenate([a(L0_xattn_Wv), np.broadcast_to(a(L0_xattn_bv), (P, d))], axis=1),
        "routing": np.concatenate([b3_rows, a(L0_ffn_gate_w).T, onehots,
                                   np.broadcast_to(np.arange(experts, 0, -1, dtype=np.float32), (P, experts))],
                                  axis=1),
        "sw12_t": sw12.transpose(2, 0, 1),
        "sw3_t": a(L0_ffn_sw3).T.reshape(chunks, P, d),
        "w13_t": np.stack([a(L0_ffn_w1).transpose(0, 2, 1), a(L0_ffn_w3).transpose(0, 2, 1)], axis=2),
        "w2_t": np.concatenate([a(L0_ffn_w2).transpose(0, 2, 1), a(L0_ffn_b1)[:, :, None], a(L0_ffn_b2)[:, :, None]],
                               axis=2),
    }
    nc = bacc.Bacc("TRN2", target_bir_lowering=False, num_devices=1)
    feeds, args = {}, []
    for name, value in arrays.items():
        value = np.ascontiguousarray(value)
        feeds[f"in_{name}"] = value
        args.append(nc.dram_tensor(f"in_{name}", value.shape, _mybir.dt.from_np(value.dtype),
                                   kind="ExternalInput").ap())
    args.append(nc.dram_tensor("out_t", (d, batch * seq), _mybir.dt.float32, kind="ExternalOutput").ap())
    xattn_moe_ffn_kernel(nc, *args)
    r = run(nc, [feeds], core_ids=[0])
    return np.ascontiguousarray(r.results[0]["out_t"].T).reshape(batch, seq, d)
```

```python
from contextlib import ExitStack

import concourse.bass as bass
from concourse import mybir

F32 = mybir.dt.float32
F32R = mybir.dt.float32r
BF16 = mybir.dt.bfloat16
ALU = mybir.AluOpType
ACT = mybir.ActivationFunctionType
AX_X = mybir.AxisListType.X

P = 128
EPS = 1e-5
WARM_UP = 9
DMA = 16
PARTS, PART_ROWS = 3, 32


def xattn_moe_ffn_kernel(nc, x, ctx_t, project, value, routing, sw12_t, sw3_t, w13_t, w2_t, scores_dram, out_t):
    T = ctx_t.shape[1]
    NT = T // P
    G = 2
    HALF = T // G
    TH = NT // G
    S = 64
    E = w2_t.shape[0]
    C = sw3_t.shape[0]
    PAIRS = E // 2
    NORM = 2
    NORMS = NT // NORM
    SCALE = 1.0 / float(P) ** 0.5
    assert P == 128 and HALF == 512 and C == 2 and E == 8

    with ExitStack() as ctx:
        def sb(name, shape, dt=F32):
            return ctx.enter_context(nc.sbuf_tensor(name, shape, dt))

        def sem(name):
            return ctx.enter_context(nc.semaphore(name))

        x_sb = sb("x_sb", [P, NT, P])
        ctx_sb = sb("ctx_sb", [P, T])
        project_sb = sb("project_sb", [P, 3 * P + 2])
        wk_sb, ident_sb, wq_sb = (project_sb[:, n * P:(n + 1) * P] for n in range(3))
        bk_sb, bq_sb = (project_sb[:, 3 * P + n:3 * P + n + 1] for n in range(2))
        value_sb = sb("value_sb", [P, 2 * P])
        wv_sb, bv_sb = value_sb[:, 0:P], value_sb[:, P:2 * P]
        routing_sb = sb("routing_sb", [P, P + 3 * E])
        b3_sb = routing_sb[:, 0:P]
        gate_sb = routing_sb[:, P:P + E]
        onehots_sb = routing_sb[:, P + E:P + 2 * E]
        rank_sb = routing_sb[:, P + 2 * E:P + 3 * E]
        sw12_sb = sb("sw12_sb", [P, 2 * C, P])
        sw12_hi = sb("sw12_hi", [P, 2 * C, P], F32R)
        sw12_lo = sb("sw12_lo", [P, 2 * C, P], F32R)
        sw3_sb = sb("sw3_sb", [P, C, P])
        ident_bf = sb("ident_bf", [P, P], BF16)

        stats = sb("stats", [P, 2, NT, 6])
        mean_var = sb("mean_var", [P, 2, NT, 2])
        var_eps = sb("var_eps", [P, 2, NT])
        rstd = sb("rstd", [P, 2, NT])
        minus_half = sb("minus_half", [P, NT])
        xn1 = sb("xn1", [P, NT, P])
        xn1_t = sb("xn1_t", [P, T])
        q_t, k_t = sb("q_t", [P, T]), sb("k_t", [P, T])
        v_sb = sb("v_sb", [P, NT, P])
        x_bv = sb("x_bv", [P, NT, P])
        score_max = sb("score_max", [P, NT])
        shifted = sb("shifted", [P, NT, S])
        probs = sb("probs", [P, NT, P])
        probs_t = sb("probs_t", [P, NT, P])
        prob_sum = sb("prob_sum", [P, NT])
        prob_rsum = sb("prob_rsum", [P, NT])
        x2 = sb("x2", [P, NT, P])
        xn2 = sb("xn2", [P, NT, P])
        x2_t = sb("x2_t", [P, T])
        xn2_t = sb("xn2_t", [P, T])
        xn2_hi = sb("xn2_hi", [P, T], F32R)
        xn2_lo = sb("xn2_lo", [P, T], F32R)

        small = {n: sb("route_" + n, [P, NT, E]) for n in (
            "shifted", "exp", "score", "eq", "key", "first", "rest", "second", "mask")}
        masked_by_expert = sb("masked_by_expert", [P, E, NT])
        small["masked"] = masked_by_expert[:, :, :].rearrange("p e t -> p t e")
        per_tile = {n: sb("route_" + n, [P, NT]) for n in (
            "lmax", "sum", "rsum", "key1", "max2", "key2")}
        route = sb("route", [P, NT, P], BF16)
        route_t = sb("route_t", [P, T], BF16)
        xs_rows = sb("xs_rows", [P, NT, P])
        pick_b3 = sb("pick_b3", [P, E, P], BF16)
        b3_part = sb("b3_part", [P, P], BF16)
        b3_q1 = sb("b3_q1", [P, P], BF16)
        b3_r1 = sb("b3_r1", [P, P])
        b3_q2 = sb("b3_q2", [P, P], BF16)
        b3_r2 = sb("b3_r2", [P, P])

        warm = sb("warm", [P, HALF], BF16)
        table_load = sb("table_load", [P, 1])
        gate_act = sb("gate_act", [P, G * C, HALF])
        gated = sb("gated", [P, G * C, HALF])
        z_t = sb("z_t", [P, T])
        y_t = sb("y_t", [P, T])

        scores_t = sb("scores_t", [E * NT, P])
        score_rows = [sb(f"score_rows{p}", [P, T]) for p in range(2)]

        w13_raw = [sb(f"w13_raw{p}", [P, 2, P]) for p in range(2)]
        w13_hi = [sb(f"w13_hi{p}", [P, 2, P], F32R) for p in range(2)]
        w13_lo = [sb(f"w13_lo{p}", [P, 2, P], F32R) for p in range(2)]
        w2_sb = [sb(f"w2_sb{p}", [P, P + 2]) for p in range(2)]
        xs = [sb(f"xs{h}", [P, HALF]) for h in range(G)]
        xs_hi = [sb(f"xs_hi{h}", [P, HALF], F32R) for h in range(G)]
        xs_lo = [sb(f"xs_lo{h}", [P, HALF], F32R) for h in range(G)]
        hidden = [sb(f"hidden{h}", [P, HALF]) for h in range(G)]
        x3 = [sb(f"x3{h}", [P, HALF]) for h in range(G)]
        prod = [sb(f"prod{h}", [P, HALF]) for h in range(G)]

        bank = [ctx.enter_context(nc.psum_tensor(f"bank{i}", [P, 512], F32)) for i in range(8)]
        ps_k, ps_q = [bank[0], bank[7]], [bank[1], bank[0]]
        ps_x2t = ps_a1 = [bank[0], bank[1]]
        ps_v = ps_av = ps_a3 = [bank[2], bank[3]]
        ps_xn1t = ps_pt = ps_xn2t = ps_a2 = [bank[4], bank[5]]
        ps_z = [bank[4], bank[3]]
        ps_scores = ps_xst = [bank[6], bank[7]]
        ps_logits = bank[7][:, 0:NT * E].rearrange("p (t e) -> p t e", e=E)
        ps_route_t = bank[1][:, :].bitcast(BF16)
        ps_a2_last = [bank[4], bank[5], bank[6]]
        ps_scores_t = bank[2][0:E * NT, 0:P]
        ps_gate = lambda g, c: bank[g] if c == 0 else bank[6 + g]
        ps_up = lambda g, c: bank[2 + g] if c == 0 else bank[4 + g]

        ld = {n: sem("ld_" + n) for n in (
            "x0", "x1", "ctx0", "ctx1", "project", "value", "routing", "sw12", "sw3")}
        ld_w13 = [sem(f"ld_w13_{p}") for p in range(2)]
        ld_scores = [[sem(f"ld_scores_{p}_{h}") for h in range(G)] for p in range(2)]
        scores_stored = sem("scores_stored")
        ld_w2 = [sem(f"ld_w2_{p}") for p in range(2)]
        stored = sem("stored")
        y_last = sem("y_last")
        (kt_mm, v_mm, xn1t_mm, q_mm, scores_mm, pt_mm, av_mm, x2t_mm, xn2t_mm, logits_mm, scores_t_mm) = (
            sem(n + "_mm") for n in (
                "kt", "v", "xn1t", "q", "scores", "pt", "av", "x2t", "xn2t", "logits", "scores_t"))
        gate_mm, up_mm, route_mm, xst_mm, a1_mm, a3_mm, a2_mm = (
            sem(n + "_mm") for n in ("gate", "up", "route", "xst", "a1", "a3", "a2"))
        (ident_cast, table_loaded, kt_out, v_out, xn1t_out, q_out, exps, pt_out, x2t_out, xn2t_out) = (
            sem(n) for n in (
                "ident_cast", "table_loaded", "kt_out", "v_out", "xn1t_out", "q_out", "exps", "pt_out", "x2t_out",
                "xn2t_out"))
        (sw12_hi_out, xn2_hi_out, silus, route_exp, route_out, scores_t_out, x3_out, xs_hi_out, w_hi_out) = (
            sem(n) for n in (
                "sw12_hi_out", "xn2_hi_out", "silus", "route_exp", "route_out", "scores_t_out", "x3_out",
                "xs_hi_out", "w_hi_out"))
        (warm_ready, stat_dve, var_ready, var_eps_out, xn1_ready, smax_ready, shift_ready, psum_ready,
         rsum_ready, x2_ready, xn2_ready, xn2_lo_out) = (
            sem(n) for n in (
                "warm_ready", "stat_dve", "var_ready", "var_eps_out", "xn1_ready", "smax_ready", "shift_ready",
                "psum_ready", "rsum_ready", "x2_ready", "xn2_ready", "xn2_lo_out"))
        (route_step, route_shift, route_rows, masked_ready, gated_ready, xs_out, xs_lo_out, prod_out) = (
            sem(n) for n in (
                "route_step", "route_shift", "route_rows", "masked_ready", "gated_ready", "xs_out", "xs_lo_out",
                "prod_out"))
        (consts_ready, zeros_ready, rstd_out, xbv_out, b3_step, pick_b3_ready, sw12_lo_out, w_lo_out, y_out) = (
            sem(n) for n in (
                "consts_ready", "zeros_ready", "rstd_out", "xbv_out", "b3_step", "pick_b3_ready", "sw12_lo_out",
                "w_lo_out", "y_out"))

        tok = lambda g: slice(g * HALF, (g + 1) * HALF)
        tile = lambda t: slice(t * P, (t + 1) * P)
        tiles = lambda g: slice(g * TH, (g + 1) * TH)
        in_half = lambda t: slice((t % TH) * P, (t % TH + 1) * P)

        last_pieces = [(0, slice(0, HALF)), (1, slice(0, HALF // 2)), (1, slice(HALF // 2, HALF))]

        x_rows = x.rearrange("(t p) d -> p t d", p=P)

        block = ctx.enter_context(nc.Block())

        @block.sync
        def _(sp):
            sp.dma_start(x_sb[:, tiles(0), :], x_rows[:, tiles(0), :]).then_inc(ld["x0"], DMA)
            sp.dma_start(project_sb[:], project).then_inc(ld["project"], DMA)
            sp.dma_start(ctx_sb[:, tok(0)], ctx_t[:, tok(0)]).then_inc(ld["ctx0"], DMA)
            sp.dma_start(x_sb[:, tiles(1), :], x_rows[:, tiles(1), :]).then_inc(ld["x1"], DMA)
            sp.dma_start(value_sb[:], value).then_inc(ld["value"], DMA)
            sp.dma_start(ctx_sb[:, tok(1)], ctx_t[:, tok(1)]).then_inc(ld["ctx1"], DMA)
            sp.dma_start(routing_sb[:], routing).then_inc(ld["routing"], DMA)
            sp.dma_start(sw12_sb[:], sw12_t).then_inc(ld["sw12"], DMA)
            sp.dma_start(sw3_sb[:], sw3_t.rearrange("c h d -> h c d")).then_inc(ld["sw3"], DMA)
            for p in range(2):
                sp.dma_start(w13_raw[p][:], w13_t[p]).then_inc(ld_w13[p], DMA)
            sp.dma_start(w2_sb[0][:], w2_t[0]).then_inc(ld_w2[0], DMA)
            sp.wait_ge(scores_t_out, 1)
            sp.dma_start(scores_dram.rearrange("e (t p) -> (e t) p", p=P), scores_t[:]).then_inc(scores_stored, DMA)
            sp.wait_ge(scores_stored, DMA)

            def spread_scores(e, p, h):
                sp.dma_start(score_rows[p][:, tok(h)], scores_dram[e, tok(h)].to_broadcast([P, HALF])
                             ).then_inc(ld_scores[p][h], DMA)

            for h in range(G):
                spread_scores(slice(1, 2), 1, h)
            with sp.Fori(0, PAIRS - 1) as i:
                for p in range(2):
                    for h in range(G):
                        sp.wait_ge(xs_out, 4 * i + 2 * p + h + 1)
                        spread_scores(bass.ds(2 * i + p + 2, 1), p, h)
                    sp.wait_ge(w_lo_out, 2 * i + p + 1)
                    sp.dma_start(w13_raw[p][:], w13_t[bass.ds(2 * i + p + 2, 1)].rearrange("o d c h -> (o d) c h")
                                 ).then_inc(ld_w13[p], DMA)
                    sp.wait_ge(prod_out, G + 4 * i + 2 * p)
                    sp.dma_start(w2_sb[1 - p][:], w2_t[bass.ds(2 * i + p + 1, 1)].rearrange("o h d -> (o h) d")
                                 ).then_inc(ld_w2[1 - p], DMA)
            sp.wait_ge(prod_out, G + 2 * (E - 2))
            sp.dma_start(w2_sb[1][:], w2_t[E - 1]).then_inc(ld_w2[1], DMA)
            for n, (h, cols) in enumerate(last_pieces):
                out_cols = slice(h * HALF + cols.start, h * HALF + cols.stop)
                sp.wait_ge(y_last, n + 1)
                sp.dma_start(out_t[:, out_cols], y_t[:, out_cols]).then_inc(stored, DMA)
            sp.wait_ge(stored, DMA * len(last_pieces))

        @block.gpsimd
        def _(pool):
            nc.gpsimd.memset(minus_half[:], -0.5).then_inc(consts_ready, 1)
            nc.gpsimd.memset(probs[:], 0.0).then_inc(zeros_ready, 1)
            nc.gpsimd.memset(route[:], 0.0).then_inc(zeros_ready, 1)

            def rsqrt_var(norm, n):
                pool.wait_ge(var_eps_out, NORMS * norm + n + 1)
                pool.wait_ge(consts_ready, 1)
                group = slice(n * NORM, (n + 1) * NORM)
                nc.gpsimd.tensor_tensor(rstd[:, norm, group], var_eps[:, norm, group], minus_half[:, group],
                                        ALU.pow).then_inc(rstd_out, 1)

            for n in range(NORMS):
                rsqrt_var(0, n)
            pool.wait_ge(ld["value"], DMA)
            for g in range(G):
                pool.wait_ge(ld[f"x{g}"], DMA)
                nc.gpsimd.tensor_tensor(x_bv[:, tiles(g), :], x_sb[:, tiles(g), :],
                                        bv_sb.unsqueeze(1).to_broadcast([P, TH, P]), ALU.add
                                        ).then_inc(xbv_out, 1)
            pool.wait_ge(ld["routing"], DMA)
            nc.gpsimd.tensor_copy(b3_q1[:], b3_sb).then_inc(b3_step, 1)
            pool.wait_ge(b3_step, 1)
            nc.gpsimd.tensor_tensor(b3_r1[:], b3_sb, b3_q1[:], ALU.subtract).then_inc(b3_step, 1)
            pool.wait_ge(b3_step, 2)
            nc.gpsimd.tensor_copy(b3_q2[:], b3_r1[:]).then_inc(b3_step, 1)
            pool.wait_ge(b3_step, 3)
            nc.gpsimd.tensor_tensor(b3_r2[:], b3_r1[:], b3_q2[:], ALU.subtract).then_inc(b3_step, 1)
            pool.wait_ge(b3_step, 4)
            nc.gpsimd.tensor_copy(b3_part[:], b3_r2[:]).then_inc(b3_step, 1)
            pool.wait_ge(b3_step, 5)
            nc.gpsimd.tensor_copy(b3_part[0:PART_ROWS, :], b3_q1[0:PART_ROWS, :]).then_inc(b3_step, 1)
            nc.gpsimd.tensor_copy(b3_part[PART_ROWS:2 * PART_ROWS, :], b3_q2[PART_ROWS:2 * PART_ROWS, :]
                                  ).then_inc(b3_step, 1)
            pool.wait_ge(b3_step, 7)
            nc.gpsimd.tensor_tensor(pick_b3[:], b3_part[:, :].unsqueeze(1).to_broadcast([P, E, P]),
                                    onehots_sb.unsqueeze(2).to_broadcast([P, E, P]), ALU.mult
                                    ).then_inc(pick_b3_ready, 1)
            for n in range(NORMS // 2):
                rsqrt_var(1, n)
            pool.wait_ge(sw12_hi_out, 1)
            nc.gpsimd.tensor_tensor(sw12_lo[:], sw12_sb[:], sw12_hi[:].bitcast(F32), ALU.subtract
                                    ).then_inc(sw12_lo_out, 1)
            for n in range(NORMS // 2, NORMS):
                rsqrt_var(1, n)

            def split_low(e, p):
                pool.wait_ge(w_hi_out, e + 1)
                nc.gpsimd.tensor_tensor(w13_lo[p][:], w13_raw[p][:], w13_hi[p][:].bitcast(F32), ALU.subtract
                                        ).then_inc(w_lo_out, 1)

            split_low(0, 0)
            for g in range(G):
                pool.wait_ge(prod_out, g + 1)
                pool.wait_ge(x2t_out, g + 1)
                nc.gpsimd.tensor_tensor(y_t[:, tok(g)], x2_t[:, tok(g)], z_t[:, tok(g)], ALU.add).then_inc(y_out, 1)

            split_low(1, 1)

            def add_pair(i, last):
                for p in range(2):
                    for h in range(G):
                        s = 4 * i + 2 * p + h
                        if last and p == 1:
                            continue
                        if h == 1 and not last:
                            split_low(2 * i + p + 2, p)
                        pool.wait_ge(prod_out, G + s + 1)
                        pool.wait_ge(y_out, s + 1)
                        nc.gpsimd.tensor_tensor(y_t[:, tok(h)], y_t[:, tok(h)], prod[h][:], ALU.add
                                                ).then_inc(y_out, 1)

            with pool.Fori(0, PAIRS - 1) as i:
                add_pair(i, False)
            add_pair(PAIRS - 1, True)

        @block.scalar
        def _(act):
            act.wait_ge(ld["project"], DMA)
            nc.scalar.activation(ident_bf[:], ident_sb, ACT.Copy).then_inc(ident_cast, 1)

            def evac_k(g):
                act.wait_ge(kt_mm, g + 1)
                nc.scalar.activation(k_t[:, tok(g)], ps_k[g][:], ACT.Identity, bias=bk_sb
                                     ).then_inc(kt_out, 1)

            def evac_v(g):
                act.wait_ge(v_mm, g + 1)
                nc.scalar.activation(v_sb[:, tiles(g), :], ps_v[g][:].rearrange("p (t d) -> p t d", d=P), ACT.Copy
                                     ).then_inc(v_out, 1)

            def evac_xn1t(g):
                act.wait_ge(xn1t_mm, g + 1)
                nc.scalar.activation(xn1_t[:, tok(g)], ps_xn1t[g][:], ACT.Copy).then_inc(xn1t_out, 1)

            def evac_q(g):
                act.wait_ge(q_mm, g + 1)
                nc.scalar.activation(q_t[:, tok(g)], ps_q[g][:], ACT.Identity, bias=bq_sb
                                     ).then_inc(q_out, 1)

            def exp_scores(g):
                act.wait_ge(shift_ready, g + 1)
                for b in range(2):
                    rows = slice(b * S, (b + 1) * S)
                    nc.scalar.activation(probs[rows, tiles(g), rows], shifted[rows, tiles(g), :], ACT.Exp,
                                         scale=SCALE).then_inc(exps, 1)

            def evac_pt(g):
                act.wait_ge(pt_mm, g + 1)
                nc.scalar.activation(probs_t[:, tiles(g), :], ps_pt[g][:].rearrange("p (t d) -> p t d", d=P), ACT.Copy
                                     ).then_inc(pt_out, 1)

            def evac_xn2t(g):
                act.wait_ge(xn2t_mm, g + 1)
                nc.scalar.activation(xn2_t[:, tok(g)], ps_xn2t[g][:], ACT.Copy).then_inc(xn2t_out, 1)

            def round_xn2t(g):
                act.wait_ge(xn2t_mm, g + 1)
                nc.scalar.activation(xn2_hi[:, tok(g)], ps_xn2t[g][:], ACT.Copy).then_inc(xn2_hi_out, 1)

            def evac_x2t(g):
                act.wait_ge(x2t_mm, g + 1)
                nc.scalar.activation(x2_t[:, tok(g)], ps_x2t[g][:], ACT.Copy).then_inc(x2t_out, 1)

            evac_xn1t(0)
            evac_k(0)
            evac_q(0)
            evac_k(1)
            evac_xn1t(1)
            act.wait_ge(zeros_ready, 1)
            exp_scores(0)
            evac_v(0)
            evac_q(1)
            evac_pt(0)
            act.wait_ge(ld["sw12"], DMA)
            nc.scalar.activation(sw12_hi[:], sw12_sb[:], ACT.Copy).then_inc(sw12_hi_out, 1)
            exp_scores(1)
            evac_v(1)
            evac_pt(1)

            def shared_silu(g, c):
                act.wait_ge(gate_mm, C * g + c + 1)
                nc.scalar.activation(gate_act[:, C * g + c, :], ps_gate(g, c)[:], ACT.Silu).then_inc(silus, 1)

            evac_x2t(0)
            round_xn2t(0)
            evac_xn2t(0)
            evac_x2t(1)
            shared_silu(0, 0)
            shared_silu(0, 1)
            evac_xn2t(1)
            round_xn2t(1)
            nc.scalar.activation(table_load[:], ident_bf[:, 0:1], ACT.Exp).then_inc(table_loaded, 1)
            act.wait_ge(route_shift, 1)
            nc.scalar.activation(small["exp"][:], small["shifted"][:], ACT.Exp).then_inc(route_exp, 1)

            def split_high(e, p, loads):
                act.wait_ge(ld_w13[p], loads)
                nc.scalar.activation(w13_hi[p][:], w13_raw[p][:], ACT.Copy).then_inc(w_hi_out, 1)

            for c in range(C):
                shared_silu(1, c)
            split_high(0, 0, DMA)
            act.wait_ge(scores_t_mm, 1)
            nc.scalar.activation(scores_t[:], ps_scores_t, ACT.Copy).then_inc(scores_t_out, 1)

            def round_xs(s, h):
                act.wait_ge(xs_out, s + 1)
                nc.scalar.activation(xs_hi[h][:], xs[h][:], ACT.Copy).then_inc(xs_hi_out, 1)

            def round_xst(h):
                act.wait_ge(xst_mm, h + 1)
                nc.scalar.activation(xs_hi[h][:], ps_xst[h][:], ACT.Copy).then_inc(xs_hi_out, 1)

            round_xst(0)
            act.wait_ge(route_mm, 1)
            for g in range(G):
                nc.scalar.activation(route_t[:, tok(g)], ps_route_t[:, tok(g)], ACT.Copy).then_inc(route_out, 1)
            round_xst(1)

            def expert_pair(i, last):
                for p in range(2):
                    e = 2 * i + p
                    for h in range(G):
                        s = 4 * i + 2 * p + h
                        if h == 0:
                            act.wait_ge(ld_w2[p], DMA * (i + 1))
                        act.wait_ge(a1_mm, s + 1)
                        act.wait_ge(a2_mm, s + 1)
                        nc.scalar.activation(hidden[h][:], ps_a1[h][:], ACT.Silu,
                                             bias=w2_sb[p][:, P:P + 1]).then_inc(silus, 1)
                        if h == 0 and not (last and p == 1):
                            split_high(e + 1, 1 - p, DMA * (i + 1 + p))
                        act.wait_ge(a3_mm, s + 1)
                        if not (last and p == 1):
                            round_xs(s + 2, h)
                        act.wait_ge(prod_out, s + 1)
                        nc.scalar.activation(x3[h][:], ps_a3[h][:], ACT.Copy).then_inc(x3_out, 1)

            with act.Fori(0, PAIRS - 1) as i:
                expert_pair(i, False)
            expert_pair(PAIRS - 1, True)

        @block.vector
        def _(dve):
            def stats_of(norm, t, src):
                nc.vector.bn_stats(stats[:, norm, t, :], src[:, t, :]).then_inc(stat_dve, 1)

            def aggregate(norm, n):
                for t in range(n * NORM, (n + 1) * NORM):
                    dve.wait_ge(stat_dve, norm * NT + t + 1)
                    last = nc.vector.bn_aggr(mean_var[:, norm, t, :], stats[:, norm, t, :])
                last.then_inc(var_ready, 1)

            def add_eps(norm, n):
                dve.wait_ge(var_ready, NORMS * norm + n + 1)
                group = slice(n * NORM, (n + 1) * NORM)
                nc.vector.tensor_scalar(var_eps[:, norm, group], mean_var[:, norm, group, 1], EPS, None,
                                        ALU.add).then_inc(var_eps_out, 1)

            def normalise(norm, n, src, dst, ready):
                dve.wait_ge(rstd_out, NORMS * norm + n + 1)
                for t in range(n * NORM, (n + 1) * NORM):
                    nc.vector.tensor_scalar(dst[:, t, :], src[:, t, :], mean_var[:, norm, t, 0:1],
                                            rstd[:, norm, t:t + 1], ALU.subtract, ALU.mult).then_inc(ready, 1)

            nc.vector.memset(warm[:], 0.0).then_inc(warm_ready, 1)

            for g in range(G):
                dve.wait_ge(ld[f"x{g}"], DMA)
                for t in range(g * TH, (g + 1) * TH):
                    stats_of(0, t, x_sb)
                    if t % TH == TH - 2:
                        aggregate(0, 2 * g)
                add_eps(0, 2 * g)
                aggregate(0, 2 * g + 1)
                add_eps(0, 2 * g + 1)
                normalise(0, 2 * g, x_sb, xn1, xn1_ready)
                normalise(0, 2 * g + 1, x_sb, xn1, xn1_ready)

            def shift_scores(g):
                scores = ps_scores[g][:, 0:TH * S].rearrange("p (t k) -> p t k", k=S)
                dve.wait_ge(scores_mm, g + 1)
                nc.vector.reduce_max(score_max[:, tiles(g)], scores, AX_X).then_inc(smax_ready, 1)
                dve.wait_ge(smax_ready, g + 1)
                nc.vector.tensor_tensor(shifted[:, tiles(g), :], scores,
                                        score_max[:, tiles(g)].unsqueeze(2).to_broadcast([P, TH, S]),
                                        ALU.subtract).then_inc(shift_ready, 1)

            def sum_probs(g, b):
                rows = slice(b * S, (b + 1) * S)
                dve.wait_ge(exps, 2 * g + b + 1)
                nc.vector.reduce_sum(prob_sum[rows, tiles(g)], probs[rows, tiles(g), rows], AX_X
                                     ).then_inc(psum_ready, 1)

            def invert_sums(g):
                dve.wait_ge(psum_ready, 2 * g + 2)
                nc.vector.reciprocal(prob_rsum[:, tiles(g)], prob_sum[:, tiles(g)]).then_inc(rsum_ready, 1)

            def attended(g, *places):
                dve.wait_ge(rsum_ready, g + 1)
                dve.wait_ge(xbv_out, g + 1)
                dve.wait_ge(av_mm, g + 1)
                for t in (g * TH + place for place in places):
                    nc.vector.scalar_tensor_tensor(out=x2[:, t, :], in0=ps_av[g][:, in_half(t)],
                                                   scalar=prob_rsum[:, t:t + 1], in1=x_bv[:, t, :],
                                                   op0=ALU.mult, op1=ALU.add).then_inc(x2_ready, 1)

            def stats_2(n):
                for t in range(n * NORM, (n + 1) * NORM):
                    dve.wait_ge(x2_ready, t + 1)
                    stats_of(1, t, x2)

            def split_xn2(g):
                dve.wait_ge(xn2t_out, g + 1)
                dve.wait_ge(xn2_hi_out, g + 1)
                nc.vector.tensor_tensor(xn2_lo[:, tok(g)], xn2_t[:, tok(g)], xn2_hi[:, tok(g)].bitcast(F32),
                                        ALU.subtract).then_inc(xn2_lo_out, 1)

            shift_scores(0)
            sum_probs(0, 0)
            sum_probs(0, 1)
            invert_sums(0)
            shift_scores(1)
            attended(0, 0, 1, 2)
            stats_2(0)
            attended(0, 3)
            aggregate(1, 0)
            stats_2(1)
            add_eps(1, 0)
            aggregate(1, 1)
            sum_probs(1, 0)
            add_eps(1, 1)
            sum_probs(1, 1)
            normalise(1, 0, x2, xn2, xn2_ready)
            invert_sums(1)
            normalise(1, 1, x2, xn2, xn2_ready)
            attended(1, 0, 1, 2)
            stats_2(2)
            attended(1, 3)
            aggregate(1, 2)
            stats_2(3)
            add_eps(1, 2)
            aggregate(1, 3)
            add_eps(1, 3)
            split_xn2(0)
            normalise(1, 2, x2, xn2, xn2_ready)
            normalise(1, 3, x2, xn2, xn2_ready)

            def shared_product(g, c):
                n = C * g + c
                dve.wait_ge(silus, n + 1)
                dve.wait_ge(up_mm, n + 1)
                nc.vector.tensor_tensor(gated[:, n, :], gate_act[:, n, :], ps_up(g, c)[:], ALU.mult
                                        ).then_inc(gated_ready, 1)

            steps = [0]

            def step(ins):
                steps[0] += 1
                ins.then_inc(route_step, 1)
                return steps[0]

            def after(n):
                dve.wait_ge(route_step, n)

            def over_experts(a):
                return a[:, :].unsqueeze(2).to_broadcast([P, NT, E])

            def first_of_equals(key, hot, eq_done):
                after(eq_done)
                n = step(nc.vector.tensor_tensor(small["key"][:], small["eq"][:], ranks, ALU.mult))
                after(n)
                n = step(nc.vector.reduce_max(key[:], small["key"][:], AX_X))
                after(n)
                return step(nc.vector.tensor_tensor(hot[:], small["key"][:], over_experts(key), ALU.is_equal))

            shared_product(0, 0)
            shared_product(0, 1)
            split_xn2(1)
            ranks = rank_sb.unsqueeze(1).to_broadcast([P, NT, E])
            dve.wait_ge(ld["routing"], DMA)
            dve.wait_ge(logits_mm, NT)
            n = step(nc.vector.reduce_max(per_tile["lmax"][:], ps_logits, AX_X))
            after(n)
            nc.vector.tensor_tensor(small["shifted"][:], ps_logits, over_experts(per_tile["lmax"]), ALU.subtract
                                    ).then_inc(route_shift, 1)
            logits_read = step(nc.vector.tensor_tensor(small["eq"][:], ps_logits, over_experts(per_tile["lmax"]),
                                                       ALU.is_equal))
            first = first_of_equals(per_tile["key1"], small["first"], logits_read)
            dve.wait_ge(route_exp, 1)
            after(first)
            rest = step(nc.vector.scalar_tensor_tensor(out=small["rest"][:], in0=small["first"][:], scalar=-2.0,
                                                       in1=small["exp"][:], op0=ALU.mult, op1=ALU.add))
            total = step(nc.vector.reduce_sum(per_tile["sum"][:], small["exp"][:], AX_X))
            after(rest)
            top = step(nc.vector.reduce_max(per_tile["max2"][:], small["rest"][:], AX_X))
            after(total)
            inverse = step(nc.vector.reciprocal(per_tile["rsum"][:], per_tile["sum"][:]))
            after(top)
            equal = step(nc.vector.tensor_tensor(small["eq"][:], small["rest"][:], over_experts(per_tile["max2"]),
                                                 ALU.is_equal))
            after(inverse)
            step(nc.vector.tensor_tensor(small["score"][:], small["exp"][:], over_experts(per_tile["rsum"]), ALU.mult))
            second = first_of_equals(per_tile["key2"], small["second"], equal)
            after(second)
            n = step(nc.vector.tensor_tensor(small["mask"][:], small["first"][:], small["second"][:], ALU.add))
            dve.wait_ge(zeros_ready, 2)
            nc.vector.tensor_tensor(route[:, :, :].rearrange("p t (q c) -> p t q c", c=PART_ROWS)[:, :, 0:PARTS, 0:E],
                                    small["first"][:, :, :].unsqueeze(2).to_broadcast([P, NT, PARTS, E]),
                                    small["second"][:, :, :].unsqueeze(2).to_broadcast([P, NT, PARTS, E]), ALU.add
                                    ).then_inc(route_rows, 1)
            after(n)
            nc.vector.tensor_tensor(small["masked"], small["score"][:], small["mask"][:], ALU.mult
                                    ).then_inc(masked_ready, 1)

            def evac_z(g):
                dve.wait_ge(a2_mm, g + 1)
                nc.vector.tensor_copy(z_t[:, tok(g)], ps_z[g][:]).then_inc(prod_out, 1)

            def scale_tokens(h, scores):
                nc.vector.tensor_tensor(xs[h][:], xn2_t[:, tok(h)], scores, ALU.mult).then_inc(xs_out, 1)

            def scale_rows(g):
                for t in range(g * TH, (g + 1) * TH):
                    ins = nc.vector.tensor_scalar(xs_rows[:, t, :], xn2[:, t, :], masked_by_expert[:, 0, t:t + 1],
                                                  None, ALU.mult)
                ins.then_inc(xs_out, 1)

            def split_xst(h):
                dve.wait_ge(xst_mm, h + 1)
                dve.wait_ge(xs_hi_out, h + 1)
                nc.vector.tensor_tensor(xs_lo[h][:], ps_xst[h][:], xs_hi[h][:].bitcast(F32), ALU.subtract
                                        ).then_inc(xs_lo_out, 1)

            def split_xs(s, h):
                dve.wait_ge(xs_hi_out, s + 1)
                nc.vector.tensor_tensor(xs_lo[h][:], xs[h][:], xs_hi[h][:].bitcast(F32), ALU.subtract
                                        ).then_inc(xs_lo_out, 1)

            dve.wait_ge(masked_ready, 1)
            scale_rows(0)
            scale_rows(1)
            shared_product(1, 0)
            shared_product(1, 1)
            split_xst(0)
            evac_z(0)
            split_xst(1)
            evac_z(1)
            dve.wait_ge(ld_scores[1][0], DMA)
            scale_tokens(0, score_rows[1][:, tok(0)])

            def expert_pair(i, last):
                for p in range(2):
                    for h in range(G):
                        s = 4 * i + 2 * p + h
                        if not (last and p == 1):
                            dve.wait_ge(a3_mm, s + 1)
                            split_xs(s + 2, h)
                        if h == 0 and not (last and p == 1):
                            dve.wait_ge(xs_lo_out, s + 2)
                            dve.wait_ge(ld_scores[1 - p][1], DMA * (i + 1))
                            scale_tokens(1, score_rows[1 - p][:, tok(1)])
                        if h == 1 and not last:
                            dve.wait_ge(xs_lo_out, s + 2)
                            dve.wait_ge(ld_scores[p][0], DMA * (i + 1 + p))
                            scale_tokens(0, score_rows[p][:, tok(0)])
                        if h == 0:
                            dve.wait_ge(ld_w2[p], DMA * (i + 1))
                        if last and p == 1:
                            continue
                        dve.wait_ge(a2_mm, G + s + 1)
                        dve.wait_ge(x3_out, s + 1)
                        dve.wait_ge(y_out, s + 1)
                        nc.vector.scalar_tensor_tensor(out=prod[h][:], in0=ps_a2[h][:],
                                                       scalar=w2_sb[p][:, P + 1:P + 2], in1=x3[h][:],
                                                       op0=ALU.add, op1=ALU.mult).then_inc(prod_out, 1)

            with dve.Fori(0, PAIRS - 1) as i:
                expert_pair(i, False)
            expert_pair(PAIRS - 1, True)
            steps_before = G * (E - 1)
            dve.wait_ge(ld_w2[1], DMA * PAIRS)

            def last_product(n):
                h, cols = last_pieces[n]
                dve.wait_ge(a2_mm, G + steps_before + n + 1)
                dve.wait_ge(x3_out, steps_before + h + 1)
                dve.wait_ge(y_out, steps_before + h + 1)
                nc.vector.scalar_tensor_tensor(out=prod[h][:, cols], in0=ps_a2_last[n][:, cols],
                                               scalar=w2_sb[1][:, P + 1:P + 2], in1=x3[h][:, cols],
                                               op0=ALU.add, op1=ALU.mult).then_inc(prod_out, 1)

            def last_sum(n):
                h, cols = last_pieces[n]
                y_cols = y_t[:, h * HALF + cols.start:h * HALF + cols.stop]
                dve.wait_ge(prod_out, G + steps_before + n + 1)
                nc.vector.tensor_tensor(y_cols, y_cols, prod[h][:, cols], ALU.add).then_inc(y_last, 1)

            last_product(0)
            last_sum(0)
            last_product(1)
            last_product(2)
            last_sum(1)
            last_sum(2)

        @block.tensor
        def _(pe):
            def mm(out, lhs_t, rhs, start=True, stop=True):
                return nc.tensor.matmul(out, lhs_t, rhs, start=start, stop=stop)

            def keys(g):
                pe.wait_ge(ld["project"], DMA)
                pe.wait_ge(ld[f"ctx{g}"], DMA)
                mm(ps_k[g][:], wk_sb, ctx_sb[:, tok(g)]).then_inc(kt_mm, 1)

            def values(g, first, end):
                pe.wait_ge(ld["value"], DMA)
                pe.wait_ge(ld[f"ctx{g}"], DMA)
                for t in range(g * TH + first, g * TH + end):
                    last = mm(ps_v[g][:, in_half(t)], ctx_sb[:, tile(t)], wv_sb)
                if end == TH:
                    last.then_inc(v_mm, 1)

            def transposes(g, src, ready, dst, done):
                for t in range(g * TH, (g + 1) * TH):
                    pe.wait_ge(ready, t + 1)
                    last = nc.tensor.transpose(dst[g][:, in_half(t)], src[:, t, :], ident_sb)
                last.then_inc(done, 1)

            def queries(g):
                pe.wait_ge(xn1t_out, g + 1)
                if g == 1:
                    pe.wait_ge(kt_out, 1)
                mm(ps_q[g][:], wq_sb, xn1_t[:, tok(g)]).then_inc(q_mm, 1)

            def scores(g):
                pe.wait_ge(q_out, g + 1)
                pe.wait_ge(kt_out, g + 1)
                for t in range(g * TH, (g + 1) * TH):
                    for b in range(2):
                        seq = slice(t * P + b * S, t * P + (b + 1) * S)
                        last = mm(ps_scores[g][b * S:(b + 1) * S, (t % TH) * S:(t % TH + 1) * S],
                                  q_t[:, seq], k_t[:, seq])
                last.then_inc(scores_mm, 1)

            def turn_probs(g):
                pe.wait_ge(exps, 2 * g + 2)
                for t in range(g * TH, (g + 1) * TH):
                    last = nc.tensor.transpose(ps_pt[g][:, in_half(t)], probs[:, t, :], ident_sb)
                last.then_inc(pt_mm, 1)

            def attend(g):
                pe.wait_ge(pt_out, g + 1)
                pe.wait_ge(v_out, g + 1)
                for t in range(g * TH, (g + 1) * TH):
                    last = mm(ps_av[g][:, in_half(t)], probs_t[:, t, :], v_sb[:, t, :])
                last.then_inc(av_mm, 1)

            def logits(g):
                pe.wait_ge(xn2t_out, g + 1)
                if g == 0:
                    pe.wait_ge(ld["routing"], DMA)
                for t in range(g * TH, (g + 1) * TH):
                    mm(ps_logits[:, t, :], xn2_t[:, tile(t)], gate_sb).then_inc(logits_mm, 1)

            def shared_high(out, n, g):
                mm(out, sw12_hi[:, n, :], xn2_hi[:, tok(g)], start=True, stop=False)
                mm(out, sw12_lo[:, n, :], xn2_hi[:, tok(g)], start=False, stop=False)

            def shared_low(out, n, g, done):
                pe.wait_ge(xn2_lo_out, g + 1)
                mm(out, sw12_hi[:, n, :], xn2_lo[:, tok(g)], start=False, stop=True).then_inc(done, 1)

            def shared_down(g, c):
                pe.wait_ge(gated_ready, C if g == 0 else C * g + c + 1)
                ins = mm(ps_z[g][:], sw3_sb[:, c, :], gated[:, C * g + c, :], start=(c == 0), stop=(c == C - 1))
                if c == C - 1:
                    ins.then_inc(a2_mm, 1)

            def turn_scaled(g):
                pe.wait_ge(xs_out, g + 1)
                for t in range(g * TH, (g + 1) * TH):
                    last = nc.tensor.transpose(ps_xst[g][:, in_half(t)], xs_rows[:, t, :], ident_sb)
                last.then_inc(xst_mm, 1)

            def stay_warm(times, b):
                for _ in range(times):
                    mm(bank[b][:], warm[:, 0:P], warm[:])

            pe.wait_ge(warm_ready, 1)
            stay_warm(WARM_UP, 7)
            keys(0)
            transposes(0, xn1, xn1_ready, ps_xn1t, xn1t_mm)
            values(0, 0, TH - 1)
            queries(0)
            keys(1)
            scores(0)
            values(0, TH - 1, TH)
            transposes(1, xn1, xn1_ready, ps_xn1t, xn1t_mm)
            queries(1)
            turn_probs(0)
            values(1, 0, 2)
            scores(1)
            attend(0)
            values(1, 2, TH)
            turn_probs(1)
            attend(1)
            transposes(0, x2, x2_ready, ps_x2t, x2t_mm)
            transposes(0, xn2, xn2_ready, ps_xn2t, xn2t_mm)
            pe.wait_ge(shift_ready, G)
            stay_warm(2, 6)
            pe.wait_ge(xn2_hi_out, 1)
            pe.wait_ge(sw12_lo_out, 1)
            pe.wait_ge(x2t_out, 1)
            shared_high(ps_gate(0, 0)[:], 0, 0)
            shared_high(ps_gate(0, 1)[:], 1, 0)
            transposes(1, x2, x2_ready, ps_x2t, x2t_mm)
            logits(0)
            shared_low(ps_gate(0, 0)[:], 0, 0, gate_mm)
            shared_low(ps_gate(0, 1)[:], 1, 0, gate_mm)
            shared_high(ps_up(0, 0)[:], C, 0)
            shared_low(ps_up(0, 0)[:], C, 0, up_mm)
            transposes(1, xn2, xn2_ready, ps_xn2t, xn2t_mm)
            shared_high(ps_up(0, 1)[:], C + 1, 0)
            shared_low(ps_up(0, 1)[:], C + 1, 0, up_mm)
            logits(1)
            pe.wait_ge(x2t_out, 2)
            pe.wait_ge(xn2_hi_out, 2)
            shared_high(ps_gate(1, 0)[:], 0, 1)
            shared_low(ps_gate(1, 0)[:], 0, 1, gate_mm)
            pe.wait_ge(route_step, 2)
            shared_high(ps_gate(1, 1)[:], 1, 1)
            shared_low(ps_gate(1, 1)[:], 1, 1, gate_mm)
            for c in range(C):
                shared_high(ps_up(1, c)[:], C + c, 1)
                shared_low(ps_up(1, c)[:], C + c, 1, up_mm)
            pe.wait_ge(ld["sw3"], DMA)
            shared_down(0, 0)
            pe.wait_ge(masked_ready, 1)
            nc.tensor.transpose(ps_scores_t, masked_by_expert[:, :, :].rearrange("p e t -> p (e t)"), ident_sb
                                ).then_inc(scores_t_mm, 1)
            shared_down(0, 1)
            pe.wait_ge(silus, G * C)
            turn_scaled(0)
            pe.wait_ge(route_rows, 1)
            pe.wait_ge(ident_cast, 1)
            for t in range(NT):
                last = nc.tensor.transpose(ps_route_t[:, tile(t)], route[:, t, :], ident_bf[:])
            last.then_inc(route_mm, 1)
            turn_scaled(1)
            shared_down(1, 0)
            shared_down(1, 1)
            pe.wait_ge(pick_b3_ready, 1)

            def split_product(s, h, out, w_hi, w_lo, stop):
                pe.wait_ge(xs_hi_out, s + 1)
                mm(out, w_hi, xs_hi[h][:], start=True, stop=False)
                mm(out, w_lo, xs_hi[h][:], start=False, stop=False)
                pe.wait_ge(xs_lo_out, s + 1)
                return mm(out, w_hi, xs_lo[h][:], start=False, stop=stop)

            def up_product(s, h, p):
                split_product(s, h, ps_a1[h][:], w13_hi[p][:, 0, :], w13_lo[p][:, 0, :], True).then_inc(a1_mm, 1)

            pe.wait_ge(w_lo_out, 1)
            up_product(0, 0, 0)

            def expert_pair(i, last):
                for p in range(2):
                    e = 2 * i + p
                    for h in range(G):
                        s = 4 * i + 2 * p + h
                        pe.wait_ge(silus, C * G + s)
                        pe.wait_ge(prod_out, s + 1)
                        split_product(s, h, ps_a3[h][:], w13_hi[p][:, 1, :], w13_lo[p][:, 1, :], False)
                        pe.wait_ge(route_out, h + 1)
                        mm(ps_a3[h][:], pick_b3[:, bass.ds(e, 1), :].rearrange("p o d -> p (o d)"),
                           route_t[:, tok(h)], start=False, stop=True).then_inc(a3_mm, 1)
                        if h == 0:
                            up_product(s + 1, 1, p)
                        elif not (last and p == 1):
                            pe.wait_ge(w_lo_out, e + 2)
                            up_product(s + 1, 0, 1 - p)
                        if h == 0:
                            pe.wait_ge(ld_w2[p], DMA * (i + 1))
                        pe.wait_ge(silus, C * G + s + 1)
                        if last and p == 1:
                            for n, (piece_h, cols) in enumerate(last_pieces):
                                if piece_h == h:
                                    mm(ps_a2_last[n][:, cols], w2_sb[p][:, 0:P], hidden[h][:, cols]
                                       ).then_inc(a2_mm, 1)
                            continue
                        mm(ps_a2[h][:], w2_sb[p][:, 0:P], hidden[h][:]).then_inc(a2_mm, 1)

            with pe.Fori(0, PAIRS - 1) as i:
                expert_pair(i, False)
            expert_pair(PAIRS - 1, True)


def kernel(x, ctx_1024, L0_xattn_Wq, L0_xattn_bq, L0_xattn_Wk, L0_xattn_bk, L0_xattn_Wv, L0_xattn_bv,
           L0_ffn_gate_w, L0_ffn_w1, L0_ffn_b1, L0_ffn_w2, L0_ffn_b2, L0_ffn_w3, L0_ffn_b3,
           L0_ffn_sw1, L0_ffn_sw2, L0_ffn_sw3):
    import numpy as np
    import concourse.bacc as bacc
    from concourse import mybir as _mybir
    from concourse.bass_utils import run_bass_kernel_spmd as run

    a = np.asarray
    batch, seq, d = x.shape
    experts = L0_ffn_w1.shape[0]
    chunks = L0_ffn_sw1.shape[0] // P
    b3_rows = np.zeros((P, d), a(L0_ffn_b3).dtype)
    for p in range(PARTS):
        b3_rows[PART_ROWS * p:PART_ROWS * p + experts] = a(L0_ffn_b3)
    sw12 = np.concatenate([a(L0_ffn_sw1).reshape(chunks, P, d), a(L0_ffn_sw2).reshape(chunks, P, d)])
    onehots = np.zeros((P, experts), np.float32)
    for p in range(PARTS):
        for c in range(experts):
            onehots[PART_ROWS * p + c, c] = 1.0
    arrays = {
        "x": a(x).reshape(batch * seq, d),
        "ctx_t": a(ctx_1024).reshape(batch * seq, d).T,
        "project": np.concatenate([a(L0_xattn_Wk), np.eye(P, dtype=np.float32), a(L0_xattn_Wq),
                                   a(L0_xattn_bk)[:, None], a(L0_xattn_bq)[:, None]], axis=1),
        "value": np.concatenate([a(L0_xattn_Wv), np.broadcast_to(a(L0_xattn_bv), (P, d))], axis=1),
        "routing": np.concatenate([b3_rows, a(L0_ffn_gate_w).T, onehots,
                                   np.broadcast_to(np.arange(experts, 0, -1, dtype=np.float32), (P, experts))],
                                  axis=1),
        "sw12_t": sw12.transpose(2, 0, 1),
        "sw3_t": a(L0_ffn_sw3).T.reshape(chunks, P, d),
        "w13_t": np.stack([a(L0_ffn_w1).transpose(0, 2, 1), a(L0_ffn_w3).transpose(0, 2, 1)], axis=2),
        "w2_t": np.concatenate([a(L0_ffn_w2).transpose(0, 2, 1), a(L0_ffn_b1)[:, :, None], a(L0_ffn_b2)[:, :, None]],
                               axis=2),
    }
    nc = bacc.Bacc("TRN2", target_bir_lowering=False, num_devices=1)
    feeds, args = {}, []
    for name, value in arrays.items():
        value = np.ascontiguousarray(value)
        feeds[f"in_{name}"] = value
        args.append(nc.dram_tensor(f"in_{name}", value.shape, _mybir.dt.from_np(value.dtype),
                                   kind="ExternalInput").ap())
    args.append(nc.dram_tensor("scores_dram", (experts, batch * seq), _mybir.dt.float32, kind="Internal").ap())
    args.append(nc.dram_tensor("out_t", (d, batch * seq), _mybir.dt.float32, kind="ExternalOutput").ap())
    xattn_moe_ffn_kernel(nc, *args)
    r = run(nc, [feeds], core_ids=[0])
    return np.ascontiguousarray(r.results[0]["out_t"].T).reshape(batch, seq, d)
```
